# Optimizing a Trainium2 kernel written in Bass

```python
import numpy as np
import jax
import jax.numpy as jnp

def _softmax(x, axis=-1):
    return jax.nn.softmax(x, axis=axis)

def _gelu(x):
    return jax.nn.gelu(x, approximate=True)

def _silu(x):
    return jax.nn.silu(x)

def _sigmoid(x):
    return jax.nn.sigmoid(x)

def _layernorm(x, axis=-1, eps=1e-05):
    m = jnp.mean(x, axis=axis, keepdims=True)
    v = jnp.var(x, axis=axis, keepdims=True)
    return (x - m) / jnp.sqrt(v + eps)

def _scatter_add(tgt, idx, src, axis=0):
    return tgt.at[idx].add(src)

def _segment_sum(src, seg, n):
    return jax.ops.segment_sum(src, seg, n)
kernel_name = 'mk_xattn_seq_d2_seqx_r4_cb2633'

def setup_inputs(seed: int=0):
    np.random.seed(seed)
    _w = jnp.asarray

    def _rec_inputs():
        import jax
        import jax.numpy as jnp
        _rk = jax.random.key(seed)
        x = 7.22e-05 + 1 * jax.random.normal(jax.random.fold_in(_rk, 1), (32, 112, 512), jnp.float32)
        _lenS = 112 - jax.random.randint(jax.random.fold_in(_rk, 7), (32,), 0, max(1, 112 // 4) + 1, jnp.int32)
        _lenS2 = 375 - jax.random.randint(jax.random.fold_in(_rk, 8), (32,), 0, max(1, 375 // 4) + 1, jnp.int32)
        _ctx_2048P = jax.random.normal(jax.random.fold_in(_rk, 11), (32, 16, 512), jnp.float32)
        _ctx_2048c = jax.random.dirichlet(jax.random.fold_in(_rk, 511), 0.3 * jnp.ones((16,), jnp.float32), (32, 375))
        _ctx_2048t = jnp.einsum('bsk,bkd->bsd', _ctx_2048c, _ctx_2048P)
        _ctx_2048t = _ctx_2048t * jax.lax.rsqrt(jnp.mean(jnp.square(_ctx_2048t)) + 1e-12) * 0.953939
        ctx_2048 = 4.13588e-05 + 0.999923 * (_ctx_2048t + 0.3 * jax.random.normal(jax.random.fold_in(_rk, 611), (32, 375, 512), jnp.float32))
        _validS = jnp.arange(112)[None, :] < _lenS[:, None]
        _validS2 = jnp.arange(375)[None, :] < _lenS2[:, None]
        _causal = jnp.tril(jnp.ones((112, 112), dtype=bool))
        mask_Bx1xSxS2_ff0 = jnp.where(jnp.ones((32, 1, 112, 375), dtype=bool), 0.0, -1000000000.0).astype(jnp.float32)
        return (x, ctx_2048, mask_Bx1xSxS2_ff0)
    x, ctx_2048, mask_Bx1xSxS2_ff0 = _rec_inputs()

    def _L0_xattn_setup():
        import jax, jax.numpy as jnp
        import numpy as np
        H = 512
        NH = 32
        KVH = 8
        HD = H // NH
        GROUPS = NH // KVH
        EPS = 1e-06
        B, L, S = (4, 256, 256)

        def _gqa_forward(hidden_state, encoder_hidden_state, encoder_attention_mask, Wq, bq, Wk, bk, Wv, bv, Wo, bo, gamma, beta):
            b, l, _ = hidden_state.shape
            s = encoder_hidden_state.shape[1]
            q = hidden_state @ Wq + bq
            k = encoder_hidden_state @ Wk + bk
            v = encoder_hidden_state @ Wv + bv
            q = q.reshape(b, l, KVH, GROUPS, HD).transpose(0, 2, 3, 1, 4)
            k = k.reshape(b, s, KVH, HD).transpose(0, 2, 1, 3)
            v = v.reshape(b, s, KVH, HD).transpose(0, 2, 1, 3)
            scale = 1.0 / jnp.sqrt(jnp.asarray(HD, q.dtype))
            scores = jnp.einsum('bkgld,bksd->bkgls', q, k) * scale
            scores = scores + encoder_attention_mask[:, :, None, :, :]
            attn = jax.nn.softmax(scores, axis=-1)
            out = jnp.einsum('bkgls,bksd->bkgld', attn, v)
            out = out.transpose(0, 3, 1, 2, 4).reshape(b, l, H)
            out = out @ Wo + bo
            x = out + hidden_state
            mu = jnp.mean(x, axis=-1, keepdims=True)
            var = jnp.var(x, axis=-1, keepdims=True)
            return (x - mu) * jax.lax.rsqrt(var + EPS) * gamma + beta
        key = jax.random.key(seed)
        ks = jax.random.split(key, 12)
        sd = 0.02
        return {'hidden_state': jax.random.normal(ks[0], (B, L, H), jnp.float32), 'encoder_hidden_state': jax.random.normal(ks[1], (B, S, H), jnp.float32), 'encoder_attention_mask': jnp.zeros((B, 1, L, S), jnp.float32), 'Wq': jax.random.normal(ks[2], (H, H), jnp.float32) * sd, 'bq': jnp.zeros((H,), jnp.float32), 'Wk': jax.random.normal(ks[3], (H, KVH * HD), jnp.float32) * sd, 'bk': jnp.zeros((KVH * HD,), jnp.float32), 'Wv': jax.random.normal(ks[4], (H, KVH * HD), jnp.float32) * sd, 'bv': jnp.zeros((KVH * HD,), jnp.float32), 'Wo': jax.random.normal(ks[5], (H, H), jnp.float32) * sd, 'bo': jnp.zeros((H,), jnp.float32), 'gamma': jnp.ones((H,), jnp.float32), 'beta': jnp.zeros((H,), jnp.float32)}
    _L0_xattn_all = _L0_xattn_setup()
    _L0_xattn_in = {k: v for k, v in _L0_xattn_all.items() if k in ('Wq', 'bq', 'Wk', 'bk', 'Wv', 'bv', 'Wo', 'bo', 'gamma', 'beta')}
    del _L0_xattn_all

    def _L1_xattn_setup():
        import jax, jax.numpy as jnp
        import numpy as np
        H = 512
        NH = 32
        KVH = 8
        HD = H // NH
        GROUPS = NH // KVH
        EPS = 1e-06
        B, L, S = (4, 256, 256)

        def _gqa_forward(hidden_state, encoder_hidden_state, encoder_attention_mask, Wq, bq, Wk, bk, Wv, bv, Wo, bo, gamma, beta):
            b, l, _ = hidden_state.shape
            s = encoder_hidden_state.shape[1]
            q = hidden_state @ Wq + bq
            k = encoder_hidden_state @ Wk + bk
            v = encoder_hidden_state @ Wv + bv
            q = q.reshape(b, l, KVH, GROUPS, HD).transpose(0, 2, 3, 1, 4)
            k = k.reshape(b, s, KVH, HD).transpose(0, 2, 1, 3)
            v = v.reshape(b, s, KVH, HD).transpose(0, 2, 1, 3)
            scale = 1.0 / jnp.sqrt(jnp.asarray(HD, q.dtype))
            scores = jnp.einsum('bkgld,bksd->bkgls', q, k) * scale
            scores = scores + encoder_attention_mask[:, :, None, :, :]
            attn = jax.nn.softmax(scores, axis=-1)
            out = jnp.einsum('bkgls,bksd->bkgld', attn, v)
            out = out.transpose(0, 3, 1, 2, 4).reshape(b, l, H)
            out = out @ Wo + bo
            x = out + hidden_state
            mu = jnp.mean(x, axis=-1, keepdims=True)
            var = jnp.var(x, axis=-1, keepdims=True)
            return (x - mu) * jax.lax.rsqrt(var + EPS) * gamma + beta
        key = jax.random.key(seed)
        ks = jax.random.split(key, 12)
        sd = 0.02
        return {'hidden_state': jax.random.normal(ks[0], (B, L, H), jnp.float32), 'encoder_hidden_state': jax.random.normal(ks[1], (B, S, H), jnp.float32), 'encoder_attention_mask': jnp.zeros((B, 1, L, S), jnp.float32), 'Wq': jax.random.normal(ks[2], (H, H), jnp.float32) * sd, 'bq': jnp.zeros((H,), jnp.float32), 'Wk': jax.random.normal(ks[3], (H, KVH * HD), jnp.float32) * sd, 'bk': jnp.zeros((KVH * HD,), jnp.float32), 'Wv': jax.random.normal(ks[4], (H, KVH * HD), jnp.float32) * sd, 'bv': jnp.zeros((KVH * HD,), jnp.float32), 'Wo': jax.random.normal(ks[5], (H, H), jnp.float32) * sd, 'bo': jnp.zeros((H,), jnp.float32), 'gamma': jnp.ones((H,), jnp.float32), 'beta': jnp.zeros((H,), jnp.float32)}
    _L1_xattn_all = _L1_xattn_setup()
    _L1_xattn_in = {k: v for k, v in _L1_xattn_all.items() if k in ('Wq', 'bq', 'Wk', 'bk', 'Wv', 'bv', 'Wo', 'bo', 'gamma', 'beta')}
    del _L1_xattn_all
    return {'x': x, 'ctx_2048': ctx_2048, 'mask_Bx1xSxS2_ff0': mask_Bx1xSxS2_ff0, 'L0_xattn_Wq': _L0_xattn_in['Wq'], 'L0_xattn_bq': _L0_xattn_in['bq'], 'L0_xattn_Wk': _L0_xattn_in['Wk'], 'L0_xattn_bk': _L0_xattn_in['bk'], 'L0_xattn_Wv': _L0_xattn_in['Wv'], 'L0_xattn_bv': _L0_xattn_in['bv'], 'L0_xattn_Wo': _L0_xattn_in['Wo'], 'L0_xattn_bo': _L0_xattn_in['bo'], 'L0_xattn_gamma': _L0_xattn_in['gamma'], 'L0_xattn_beta': _L0_xattn_in['beta'], 'L1_xattn_Wq': _L1_xattn_in['Wq'], 'L1_xattn_bq': _L1_xattn_in['bq'], 'L1_xattn_Wk': _L1_xattn_in['Wk'], 'L1_xattn_bk': _L1_xattn_in['bk'], 'L1_xattn_Wv': _L1_xattn_in['Wv'], 'L1_xattn_bv': _L1_xattn_in['bv'], 'L1_xattn_Wo': _L1_xattn_in['Wo'], 'L1_xattn_bo': _L1_xattn_in['bo'], 'L1_xattn_gamma': _L1_xattn_in['gamma'], 'L1_xattn_beta': _L1_xattn_in['beta']}

def reference(x, ctx_2048, mask_Bx1xSxS2_ff0, L0_xattn_Wq, L0_xattn_bq, L0_xattn_Wk, L0_xattn_bk, L0_xattn_Wv, L0_xattn_bv, L0_xattn_Wo, L0_xattn_bo, L0_xattn_gamma, L0_xattn_beta, L1_xattn_Wq, L1_xattn_bq, L1_xattn_Wk, L1_xattn_bk, L1_xattn_Wv, L1_xattn_bv, L1_xattn_Wo, L1_xattn_bo, L1_xattn_gamma, L1_xattn_beta):
    import jax
    import jax.numpy as jnp

    def _L0_xattn_ref(hidden_state, encoder_hidden_state, encoder_attention_mask, Wq, bq, Wk, bk, Wv, bv, Wo, bo, gamma, beta):
        import jax, jax.numpy as jnp
        import numpy as np
        H = 512
        NH = 32
        KVH = 8
        HD = H // NH
        GROUPS = NH // KVH
        EPS = 1e-06
        B, L, S = (4, 256, 256)

        def _gqa_forward(hidden_state, encoder_hidden_state, encoder_attention_mask, Wq, bq, Wk, bk, Wv, bv, Wo, bo, gamma, beta):
            b, l, _ = hidden_state.shape
            s = encoder_hidden_state.shape[1]
            q = hidden_state @ Wq + bq
            k = encoder_hidden_state @ Wk + bk
            v = encoder_hidden_state @ Wv + bv
            q = q.reshape(b, l, KVH, GROUPS, HD).transpose(0, 2, 3, 1, 4)
            k = k.reshape(b, s, KVH, HD).transpose(0, 2, 1, 3)
            v = v.reshape(b, s, KVH, HD).transpose(0, 2, 1, 3)
            scale = 1.0 / jnp.sqrt(jnp.asarray(HD, q.dtype))
            scores = jnp.einsum('bkgld,bksd->bkgls', q, k) * scale
            scores = scores + encoder_attention_mask[:, :, None, :, :]
            attn = jax.nn.softmax(scores, axis=-1)
            out = jnp.einsum('bkgls,bksd->bkgld', attn, v)
            out = out.transpose(0, 3, 1, 2, 4).reshape(b, l, H)
            out = out @ Wo + bo
            x = out + hidden_state
            mu = jnp.mean(x, axis=-1, keepdims=True)
            var = jnp.var(x, axis=-1, keepdims=True)
            return (x - mu) * jax.lax.rsqrt(var + EPS) * gamma + beta
        return _gqa_forward(hidden_state, encoder_hidden_state, encoder_attention_mask, Wq, bq, Wk, bk, Wv, bv, Wo, bo, gamma, beta)

    def _L1_xattn_ref(hidden_state, encoder_hidden_state, encoder_attention_mask, Wq, bq, Wk, bk, Wv, bv, Wo, bo, gamma, beta):
        import jax, jax.numpy as jnp
        import numpy as np
        H = 512
        NH = 32
        KVH = 8
        HD = H // NH
        GROUPS = NH // KVH
        EPS = 1e-06
        B, L, S = (4, 256, 256)

        def _gqa_forward(hidden_state, encoder_hidden_state, encoder_attention_mask, Wq, bq, Wk, bk, Wv, bv, Wo, bo, gamma, beta):
            b, l, _ = hidden_state.shape
            s = encoder_hidden_state.shape[1]
            q = hidden_state @ Wq + bq
            k = encoder_hidden_state @ Wk + bk
            v = encoder_hidden_state @ Wv + bv
            q = q.reshape(b, l, KVH, GROUPS, HD).transpose(0, 2, 3, 1, 4)
            k = k.reshape(b, s, KVH, HD).transpose(0, 2, 1, 3)
            v = v.reshape(b, s, KVH, HD).transpose(0, 2, 1, 3)
            scale = 1.0 / jnp.sqrt(jnp.asarray(HD, q.dtype))
            scores = jnp.einsum('bkgld,bksd->bkgls', q, k) * scale
            scores = scores + encoder_attention_mask[:, :, None, :, :]
            attn = jax.nn.softmax(scores, axis=-1)
            out = jnp.einsum('bkgls,bksd->bkgld', attn, v)
            out = out.transpose(0, 3, 1, 2, 4).reshape(b, l, H)
            out = out @ Wo + bo
            x = out + hidden_state
            mu = jnp.mean(x, axis=-1, keepdims=True)
            var = jnp.var(x, axis=-1, keepdims=True)
            return (x - mu) * jax.lax.rsqrt(var + EPS) * gamma + beta
        return _gqa_forward(hidden_state, encoder_hidden_state, encoder_attention_mask, Wq, bq, Wk, bk, Wv, bv, Wo, bo, gamma, beta)
    x = _L0_xattn_ref(x, ctx_2048, mask_Bx1xSxS2_ff0, L0_xattn_Wq, L0_xattn_bq, L0_xattn_Wk, L0_xattn_bk, L0_xattn_Wv, L0_xattn_bv, L0_xattn_Wo, L0_xattn_bo, L0_xattn_gamma, L0_xattn_beta)
    x = _L1_xattn_ref(x, ctx_2048, mask_Bx1xSxS2_ff0, L1_xattn_Wq, L1_xattn_bq, L1_xattn_Wk, L1_xattn_bk, L1_xattn_Wv, L1_xattn_bv, L1_xattn_Wo, L1_xattn_bo, L1_xattn_gamma, L1_xattn_beta)
    return x

_drawn_inputs = setup_inputs


def setup_inputs(seed=0):
    import zlib

    import numpy as np

    out = dict(_drawn_inputs(seed))
    spreads = {'L0_xattn_bq': (0.0, 0.8),
     'L0_xattn_bk': (0.0, 0.8),
     'L0_xattn_bv': (0.0, 0.1),
     'L0_xattn_bo': (0.0, 0.1),
     'L0_xattn_gamma': (1.0, 0.2),
     'L0_xattn_beta': (0.0, 0.1),
     'L1_xattn_bq': (0.0, 0.8),
     'L1_xattn_bk': (0.0, 0.8),
     'L1_xattn_bv': (0.0, 0.1),
     'L1_xattn_bo': (0.0, 0.1),
     'L1_xattn_gamma': (1.0, 0.2),
     'L1_xattn_beta': (0.0, 0.1)}
    factors = {'L0_xattn_Wq': 7.785, 'L0_xattn_Wk': 7.647, 'L1_xattn_Wq': 7.666, 'L1_xattn_Wk': 7.548}
    for name, (base, spread) in spreads.items():
        noise = np.random.default_rng([zlib.crc32(name.encode()), seed]).standard_normal(out[name].shape)
        drawn = base * np.exp(spread * noise) if base else spread * noise
        out[name] = jnp.asarray(drawn.astype(out[name].dtype))
    for name, factor in factors.items():
        out[name] = (out[name] * factor).astype(out[name].dtype)
    return out
```

```python
import concourse.bass as bass
from concourse import mybir
from contextlib import ExitStack

F32 = mybir.dt.float32
BF16 = mybir.dt.bfloat16
U32 = mybir.dt.uint32
I32 = mybir.dt.int32
ALU = mybir.AluOpType
ACT = mybir.ActivationFunctionType
AX_X = mybir.AxisListType.X

B, S, S2, D = 32, 112, 375, 512
NH, NKV, HD = 32, 8, 16
NG = NH // NKV
LAYERS = 2
P = 128
DC = D // P
KC = 3
KCS = S2 // KC
GL = NG * S
SCALE = float(HD) ** -0.5
EPS = 1e-6
LOWEST = -3.0e38

TERMS = [(0, 0), (0, 1), (1, 0), (1, 1), (0, 2), (2, 0)]
NT = len(TERMS)
KT = NT * HD
PARTS = 3
KM = KT + PARTS

PIECES = 12
HALF = PIECES // 2
NPV = PIECES // 2
RING = 4
HEADS_AT = [0, 0, 3, 3, 3, 3, 4, 3, 3, 3, 3, 4]
HEAD0 = [sum(HEADS_AT[:k]) for k in range(PIECES + 1)]
HH = NH // 2
NSTACK = 2 * NT
assert KCS * KC == S2 and HEAD0[-1] == NH and KM <= P and HEAD0[7] == HH


def units(L, i):
    main = i if L == 0 else i - 1
    ahead = i - 1 if L == 0 else i + 1
    post = ahead - 1
    proj = main + 1
    return main, ahead, post, proj


def exists(L, i):
    if i is None:
        return True, True, True, True
    return tuple(0 <= b < B for b in units(L, i))


def need(eng, sem, value):
    if isinstance(value, int) and value <= 0:
        return
    eng.wait_ge(sem, value)


def piece(k):
    half, chunk, pair = k // HALF, (k % HALF) // 2, k % 2
    return chunk, [4 * half + 2 * pair + j for j in range(2)]


def cross_attention_two_layers(nc, xT_d, x_d, ctxT_d, mask_d, mflat_d, W, out):
    with ExitStack() as ctx:
        def sb(name, shape, dt=F32):
            return ctx.enter_context(nc.sbuf_tensor(name, shape, dt))

        def ps(name, shape, dt=F32):
            return ctx.enter_context(nc.psum_tensor(name, shape, dt))

        def sem(name):
            return ctx.enter_context(nc.semaphore(name))

        def per_layer(make, name, *a):
            return [make(f"{name}{L}", *a) for L in range(LAYERS)]

        wq = per_layer(sb, "wq", [P, DC, NG, P])
        wk = per_layer(sb, "wk", [P, DC, P])
        wv = per_layer(sb, "wv", [P, DC, P])
        wo = per_layer(sb, "wo", [P, NG, D])
        bq = per_layer(sb, "bq", [P, NG])
        bqs = per_layer(sb, "bqs", [P, NG])
        bk = per_layer(sb, "bk", [P, 1])
        bv = per_layer(sb, "bv", [KCS, P])
        bo = per_layer(sb, "bo", [S, D])
        gamma = per_layer(sb, "gamma", [S, D])
        beta = per_layer(sb, "beta", [S, D])
        ident = sb("ident", [P, P])
        ident4 = sb("ident4", [S, NG, S])
        identb = sb("identb", [S, S], BF16)
        neghalf = sb("neghalf", [S, 1])
        pause = sb("pause", [S, 1])
        mflat = sb("mflat", [P, B * S * S2 // P], U32)
        mcol = sb("mcol", [P, 1])
        mrow = sb("mrow", [1, 2])
        mflag = sb("mflag", [1, 1], I32)
        ctxT = per_layer(sb, "ctxT", [P, DC, S2])
        xT = per_layer(sb, "xT", [P, DC, S])
        xin = sb("xin", [S, D])
        mask = per_layer(sb, "mask", [S, S2])
        qf = sb("qf", [P, GL])
        qr = sb("qr", [P, GL])
        qp = sb("qp", [P, PARTS, GL], BF16)
        kf = sb("kf", [P, S2])
        kr = sb("kr", [P, S2])
        kp = sb("kp", [P, PARTS, S2], BF16)
        qs = per_layer(sb, "qs", [P, NKV, GL], BF16)
        ks = per_layer(sb, "ks", [P, NKV, S2], BF16)
        vs = per_layer(sb, "vs", [KCS, KC, NKV, HD, 2])
        scratch = sb("scratch", [S, S2], BF16)
        mx = per_layer(sb, "mx", [S, NH])
        mr = sb("mr", [S, HH])
        mp = sb("mp", [S, 2 * PARTS, HH], BF16)
        mT = sb("mT", [PARTS * HH, S], BF16)
        probs = sb("probs", [KCS, RING, 2, GL])
        oraw = [sb(f"oraw{h}", [P, GL]) for h in range(2)]
        oc = sb("oc", [P, GL])
        osum = sb("osum", [P, GL])
        orec = sb("orec", [P, GL])
        on = sb("on", [P, GL])
        res = per_layer(sb, "res", [S, D])
        tsum = sb("tsum", [S, D])
        stats = sb("stats", [S, 6])
        mv = sb("mv", [S, 2])
        veps = sb("veps", [S, 1])
        rstd = sb("rstd", [S, 1])
        z = sb("z", [S, D])
        zg = sb("zg", [S, D])
        y = per_layer(sb, "y", [S, D])

        sc = [ps(f"sc{h}", [P, 2, 512]) for h in range(2)]
        ms = [ps(f"ms{h}", [P, 512]) for h in range(2)]
        pv = ps("pv", [P, 512])
        job = ps("job", [P, 512])
        jobb = job[:, :].bitcast(BF16)

        w_in = sem("w_in")
        mf_in = sem("mf_in")
        consts = sem("consts")
        ids = sem("ids")
        idd = sem("idd")
        flag_col = sem("flag_col")
        flag_row = sem("flag_row")
        flag_ok = sem("flag_ok")
        ctx_in = per_layer(sem, "ctx_in")
        mask_in = per_layer(sem, "mask_in")
        xT_in = sem("xT_in")
        x_in = sem("x_in")
        k_ps = per_layer(sem, "k_ps")
        v_ps = per_layer(sem, "v_ps")
        q_ps = per_layer(sem, "q_ps")
        o_ps = per_layer(sem, "o_ps")
        t_ps = sem("t_ps")
        mt_ps = per_layer(sem, "mt_ps")
        k_evac = per_layer(sem, "k_evac")
        q_evac = per_layer(sem, "q_evac")
        k_p1 = per_layer(sem, "k_p1")
        k_r = per_layer(sem, "k_r")
        k_p2 = per_layer(sem, "k_p2")
        k_p3 = per_layer(sem, "k_p3")
        q_p1 = per_layer(sem, "q_p1")
        q_r = per_layer(sem, "q_r")
        q_p2 = per_layer(sem, "q_p2")
        q_p3 = per_layer(sem, "q_p3")
        v_ready = per_layer(sem, "v_ready")
        xT_ready = sem("xT_ready")
        stack = [[sem(f"stack{L}{h}") for h in range(2)] for L in range(LAYERS)]
        m_rows = [[sem(f"m_rows{L}{h}") for h in range(2)] for L in range(LAYERS)]
        ms_ps = per_layer(sem, "ms_ps")
        max_done = per_layer(sem, "max_done")
        m_part = per_layer(sem, "m_part")
        mt_evac = per_layer(sem, "mt_evac")
        sc_ps = per_layer(sem, "sc_ps")
        exp_done = per_layer(sem, "exp_done")
        pv_ps = per_layer(sem, "pv_ps")
        pv_evac = [[sem(f"pv_evac{L}{h}") for h in range(2)] for L in range(LAYERS)]
        o_in = per_layer(sem, "o_in")
        o_rec = per_layer(sem, "o_rec")
        on_ready = per_layer(sem, "on_ready")
        res_ready = per_layer(sem, "res_ready")
        o_evac = per_layer(sem, "o_evac")
        ln = per_layer(sem, "ln")
        rs_ready = per_layer(sem, "rs_ready")
        z_ready = per_layer(sem, "z_ready")
        zg_ready = per_layer(sem, "zg_ready")
        y_ready = per_layer(sem, "y_ready")
        out_done = sem("out_done")

        NW = 10 * LAYERS
        block = ctx.enter_context(nc.Block())

        @block.sync
        def _(sp):
            def load_ctx(L, b):
                sp.dma_start(ctxT[L][:, :, :].rearrange("p a b -> p (a b)"), ctxT_d[b]).then_inc(ctx_in[L], 16)

            def load_mask(L, b):
                sp.dma_start(mask[L][:, :], mask_d[b]).then_inc(mask_in[L], 16)

            def load_xT(b):
                sp.dma_start(xT[0][:, :, :].rearrange("p a b -> p (a b)"), xT_d[b]).then_inc(xT_in, 16)

            def load_x(b):
                sp.dma_start(xin[:, :], x_d[b]).then_inc(x_in, 16)

            def stack_terms(L, h, dst, src, which):
                for t, parts in enumerate(TERMS):
                    sp.dma_start(dst[HD * t:HD * t + HD, 4 * h:4 * h + 4, :].rearrange("d g n -> d (g n)"),
                                 src[64 * h:64 * h + 64, parts[which], :]).then_inc(stack[L][h], 16)

            def max_rows(L, h, count):
                need(sp, mt_evac[L], count)
                sp.dma_start(qs[L][KT:KM, 4 * h:4 * h + 4, :].rearrange("p g n -> p (g n)"), mT[:, :])\
                  .then_inc(m_rows[L][h], 16)

            def outputs(L, h, count):
                need(sp, pv_evac[L][h], count)
                for dst, r0 in ((oc, 0), (osum, 1)):
                    sp.dma_start(dst[64 * h:64 * h + 64, :], oraw[h][r0::2, :]).then_inc(o_in[L], 16)

            def slot(L, i, has):
                main, ahead, post, proj = units(L, i)
                m_ok, a_ok, p_ok, j_ok = has
                O = 1 - L

                def count(value):
                    return value if isinstance(value, int) else sp.snap(value)

                mains, projs, aheads = count(main), count(proj), count(ahead)
                projs1, aheads1 = count(proj + 1), count(ahead + 1)
                main_half2 = count(2 * main + 2)
                ahead_half1 = count(2 * ahead + 1)
                scores_half, scores_all = count(PIECES * main + HALF), count(PIECES * main + PIECES)
                if L == 0 and j_ok:
                    need(sp, q_ps[0], projs)
                    load_xT(projs)
                if L == 0 and m_ok:
                    need(sp, res_ready[0], mains)
                    load_x(mains)
                if p_ok:
                    outputs(O, 1, aheads)
                if m_ok:
                    max_rows(L, 1, main_half2)
                if a_ok and not (isinstance(ahead, int) and ahead + 1 >= B):
                    need(sp, v_ps[O], aheads1)
                    load_ctx(O, aheads1)
                if j_ok:
                    need(sp, k_p3[L], projs1)
                    need(sp, sc_ps[L], scores_half)
                    stack_terms(L, 0, ks[L], kp, 1)
                if m_ok:
                    if p_ok:
                        need(sp, on_ready[O], aheads)
                    outputs(L, 0, projs)
                if p_ok and O == 1:
                    need(sp, y_ready[1], aheads)
                    sp.dma_start(out[post], y[1][:, :]).then_inc(out_done, 16)
                if a_ok:
                    max_rows(O, 0, ahead_half1)
                if j_ok:
                    need(sp, sc_ps[L], scores_all)
                    load_mask(L, projs)
                    stack_terms(L, 1, ks[L], kp, 1)
                    need(sp, q_p3[L], projs1)
                    stack_terms(L, 0, qs[L], qp, 0)
                    stack_terms(L, 1, qs[L], qp, 0)

            def load_rows(L):
                for dst, key in ((bv, "bv"), (bo, "bo"), (gamma, "gamma"), (beta, "beta")):
                    n = dst[L].shape[0]
                    sp.dma_start(dst[L][:, :], W[L][key].to_broadcast([n, dst[L].shape[1]])).then_inc(w_in, 16)

            for L in range(LAYERS):
                sp.dma_start(wk[L][:, :, :].rearrange("p a b -> p (a b)"), W[L]["Wk"]).then_inc(w_in, 16)
                load_ctx(L, 0)
                sp.dma_start(wq[L][:, :, :, :].rearrange("p a b c -> p (a b c)"), W[L]["Wq"]).then_inc(w_in, 16)
                sp.dma_start(wv[L][:, :, :].rearrange("p a b -> p (a b)"), W[L]["Wv"]).then_inc(w_in, 16)
                sp.dma_start(wo[L][:, :, :].rearrange("p a b -> p (a b)"), W[L]["Wo"]).then_inc(w_in, 16)
                sp.dma_start(bq[L][:, :], W[L]["bq"]).then_inc(w_in, 16)
                sp.dma_start(bk[L][:, :], W[L]["bk"]).then_inc(w_in, 16)
                load_rows(L)
            sp.dma_start(mflat[:, :], mflat_d).then_inc(mf_in, 16)
            sp.wait_ge(consts, 1)
            run(sp, slot)
            sp.wait_ge(out_done, 16 * B)

        @block.gpsimd
        def _(pool):
            nc.gpsimd.memset(ident[:, :], 0.0).then_inc(ids, 1)
            nc.gpsimd.memset(ident4[:, :, :], 0.0).then_inc(ids, 1)
            nc.gpsimd.memset(neghalf[:, :], -0.5).then_inc(ids, 1)
            pool.wait_ge(ids, 3)
            nc.gpsimd.affine_select(out=ident[:, :], in_=ident[:, :], compare_op=ALU.not_equal, fill=1.0,
                                    base=0, pattern=[[-1, P]], channel_multiplier=1).then_inc(idd, 1)
            nc.gpsimd.affine_select(out=ident4[:, :, :], in_=ident4[:, :, :], compare_op=ALU.not_equal, fill=1.0,
                                    base=0, pattern=[[0, NG], [-1, S]], channel_multiplier=1).then_inc(idd, 1)

            def slot(L, i, has):
                main, ahead, post, proj = units(L, i)
                m_ok, a_ok, p_ok, j_ok = has
                O = 1 - L
                if p_ok and O == 0:
                    need(pool, x_in, 16 * (post + 1))
                    need(pool, o_evac[0], post)
                    nc.gpsimd.tensor_tensor(res[0][:, :], xin[:, :], bo[0][:, :], ALU.add).then_inc(res_ready[0], 1)
                if j_ok:
                    need(pool, k_p1[L], proj + 1)
                    nc.gpsimd.tensor_tensor(kr[:, :], kf[:, :], kp[:, 0, :], ALU.subtract).then_inc(k_r[L], 1)
                    need(pool, k_p2[L], proj + 1)
                    nc.gpsimd.tensor_tensor(kp[:, 2, :], kr[:, :], kp[:, 1, :], ALU.subtract).then_inc(k_p3[L], 1)
                if p_ok:
                    need(pool, ln[O], 3 * (post + 1))
                    nc.gpsimd.tensor_tensor(rstd[:, :], veps[:, :], neghalf[:, :], ALU.pow).then_inc(rs_ready[O], 1)
                    need(pool, z_ready[O], post + 1)
                    nc.gpsimd.tensor_tensor(zg[:, :], z[:, :], gamma[O][:, :], ALU.mult).then_inc(zg_ready[O], 1)
                    need(pool, zg_ready[O], post + 1)
                    if O == 1:
                        need(pool, out_done, 16 * post)
                    else:
                        need(pool, t_ps, post)
                        need(pool, res_ready[1], post)
                    nc.gpsimd.tensor_tensor(y[O][:, :], zg[:, :], beta[O][:, :], ALU.add).then_inc(y_ready[O], 1)
                if a_ok and O == 1:
                    need(pool, y_ready[0], ahead + 1)
                    need(pool, o_evac[1], ahead)
                    nc.gpsimd.tensor_tensor(res[1][:, :], y[0][:, :], bo[1][:, :], ALU.add).then_inc(res_ready[1], 1)
                if j_ok:
                    need(pool, q_p1[L], proj + 1)
                    nc.gpsimd.tensor_tensor(qr[:, :], qf[:, :], qp[:, 0, :], ALU.subtract).then_inc(q_r[L], 1)
                    need(pool, q_p2[L], proj + 1)
                    nc.gpsimd.tensor_tensor(qp[:, 2, :], qr[:, :], qp[:, 1, :], ALU.subtract).then_inc(q_p3[L], 1)

            pool.wait_ge(w_in, 16 * NW)
            run(pool, slot)

        @block.scalar
        def _(act):
            def slot(L, i, has):
                main, ahead, post, proj = units(L, i)
                m_ok, a_ok, p_ok, j_ok = has
                O = 1 - L

                def exp(k):
                    if not m_ok:
                        return
                    need(act, sc_ps[L], PIECES * main + k + 1)
                    if k >= RING:
                        need(act, pv_ps[L], NPV * main + (k - RING) // 2 + 1)
                    elif p_ok:
                        need(act, pv_ps[O], NPV * post + (PIECES - RING + k) // 2 + 1)
                    nc.scalar.activation(probs[:, k % RING, :, :], sc[k % 2][0:KCS, :, 0:GL], ACT.Exp)\
                      .then_inc(exp_done[L], 1)

                def pv_out(U, h, b, before):
                    need(act, pv_ps[U], NPV * b + 3 * (h + 1))
                    if before is not None:
                        need(act, o_in[before[0]], 64 * before[1] + 32 * (h + 1))
                    nc.scalar.copy(oraw[h][:, :], pv[:, 0:GL]).then_inc(pv_evac[U][h], 1)

                def m_out(U, h, b, rows):
                    need(act, mt_ps[U], 2 * b + h + 1)
                    if rows is not None:
                        need(act, m_rows[rows[0]][1 - h], 16 * rows[1])
                    nc.scalar.copy(mT[:, :], jobb[0:PARTS * HH, 0:S]).then_inc(mt_evac[U], 1)

                for k in range(PIECES):
                    exp(k)
                    if k == 1 and p_ok:
                        first, last = isinstance(main, int) and main < 1, isinstance(main, int) and main > B
                        pv_out(O, 1, post, (O, post - 1) if last else None if first else (L, main - 1))
                    if k == 2 and m_ok:
                        m_out(L, 1, main, (L, main + 1))
                    if k == 4 and j_ok:
                        need(act, k_ps[L], proj + 1)
                        if a_ok:
                            need(act, k_r[O], ahead + 1)
                            need(act, stack[O][0], 16 * NSTACK * (ahead + 1))
                            need(act, stack[O][1], 16 * NSTACK * (ahead + 1))
                        nc.scalar.activation(kf[:, :], job[:, 0:S2], ACT.Identity, bias=bk[L][:, 0:1])\
                          .then_inc(k_evac[L], 1)
                        need(act, k_evac[L], proj + 1)
                        nc.scalar.copy(kp[:, 0, :], kf[:, :]).then_inc(k_p1[L], 1)
                    if k == 5 and j_ok:
                        need(act, k_r[L], proj + 1)
                        nc.scalar.copy(kp[:, 1, :], kr[:, :]).then_inc(k_p2[L], 1)
                    if k == 7 and m_ok:
                        pv_out(L, 0, main, (O, post) if p_ok else None)
                    if k == 8 and a_ok:
                        m_out(O, 0, ahead, (L, main + 1) if m_ok else None)
                    if k == 9 and p_ok and O == 0:
                        need(act, t_ps, post + 1)
                        need(act, q_ps[1], post)
                        nc.scalar.copy(xT[1][:, :, :].rearrange("p a b -> p (a b)"), job[:, 0:GL])\
                          .then_inc(xT_ready, 1)
                    if k == 10 and j_ok:
                        need(act, q_ps[L], proj + 1)
                        if a_ok:
                            need(act, q_r[O], ahead + 1)
                        for c in range(NG):
                            nc.scalar.activation(qf[:, S * c:S * c + S], job[:, S * c:S * c + S], ACT.Identity,
                                                 bias=bqs[L][:, c:c + 1], scale=SCALE).then_inc(q_evac[L], 1)
                        need(act, q_evac[L], NG * (proj + 1))
                        nc.scalar.copy(qp[:, 0, :], qf[:, :]).then_inc(q_p1[L], 1)
                    if k == 11 and j_ok:
                        need(act, q_r[L], proj + 1)
                        nc.scalar.copy(qp[:, 1, :], qr[:, :]).then_inc(q_p2[L], 1)

            act.wait_ge(w_in, 16 * NW)
            act.wait_ge(consts, 1 + LAYERS)
            run(act, slot)

        @block.vector
        def _(dve):
            for L in range(LAYERS):
                nc.vector.memset(qs[L][:, :, :].bitcast(U32), 0)
                nc.vector.memset(ks[L][:, :, :], 1.0)
                nc.vector.memset(vs[L][:, :, :, :, 1], 1.0)
            last = nc.vector.memset(mp[:, :, :], 0.0)
            last.then_inc(consts, 1)
            dve.wait_ge(w_in, 16 * NW)
            for L in range(LAYERS):
                nc.vector.tensor_scalar(bqs[L][:, :], bq[L][:, :], SCALE, None, ALU.mult).then_inc(consts, 1)
            dve.wait_ge(idd, 2)
            nc.vector.tensor_copy(identb[:, :], ident[0:S, 0:S]).then_inc(idd, 1)
            dve.wait_ge(mf_in, 16)
            nc.vector.tensor_reduce(mcol[:, :], mflat[:, :], AX_X, ALU.max).then_inc(flag_col, 1)
            dve.wait_ge(flag_row, 1)
            nc.vector.tensor_reduce(mrow[:, 0:1], job[0:1, 0:P], AX_X, ALU.max).then_inc(flag_ok, 1)
            dve.wait_ge(flag_ok, 1)
            nc.vector.tensor_scalar(mflag[:, :], mrow[:, 0:1], 0.0, None, ALU.is_gt).then_inc(flag_ok, 1)

            def slots(masked):
                def slot(L, i, has):
                    main, ahead, post, proj = units(L, i)
                    m_ok, a_ok, p_ok, j_ok = has
                    O = 1 - L

                    def maximum(hh):
                        need(dve, ms_ps[O], NH * ahead + hh + 1)
                        if masked:
                            nc.vector.memset(pause[:, :], 0.0)
                            nc.vector.tensor_tensor_reduce(out=scratch[:, :], in0=ms[hh % 2][0:S, 0:S2],
                                                           in1=mask[O][:, :], scale=1.0, scalar=LOWEST, op0=ALU.add,
                                                           op1=ALU.max, accum_out=mx[O][:, hh:hh + 1])\
                              .then_inc(max_done[O], 1)
                        else:
                            nc.vector.tensor_reduce(mx[O][:, hh:hh + 1], ms[hh % 2][0:S, 0:S2], AX_X, ALU.max)\
                              .then_inc(max_done[O], 1)

                    def max_parts(U, h, b):
                        cols = mx[U][:, HH * h:HH * h + HH]
                        done = 4 * (2 * b + h)
                        need(dve, max_done[U], NH * b + HH * (h + 1))
                        if h == 1:
                            need(dve, mt_ps[U], 2 * b + 1)
                        elif m_ok:
                            need(dve, mt_ps[L], 2 * main + 2)
                        nc.vector.tensor_scalar(mp[:, 0, :], cols, -1.0, None, ALU.mult).then_inc(m_part[U], 1)
                        need(dve, m_part[U], done + 1)
                        nc.vector.scalar_tensor_tensor(out=mr[:, :], in0=cols, scalar=-1.0, in1=mp[:, 0, :],
                                                       op0=ALU.mult, op1=ALU.subtract).then_inc(m_part[U], 1)
                        need(dve, m_part[U], done + 2)
                        nc.vector.tensor_copy(mp[:, 1, :], mr[:, :]).then_inc(m_part[U], 1)
                        need(dve, m_part[U], done + 3)
                        nc.vector.tensor_tensor(mp[:, 2, :], mr[:, :], mp[:, 1, :], ALU.subtract)\
                          .then_inc(m_part[U], 1)

                    if m_ok:
                        max_parts(L, 1, main)
                    for k in range(PIECES):
                        if k == 3 and a_ok:
                            need(dve, v_ps[O], ahead + 1)
                            if p_ok:
                                need(dve, pv_ps[O], NPV * (post + 1))
                            nc.vector.tensor_tensor(
                                vs[O][:, :, :, :, 0], job[0:KCS, 0:KC * P].rearrange("p (c g d) -> p c g d", c=KC, d=HD),
                                bv[O][:, :].rearrange("p (g d) -> p g d", d=HD).unsqueeze(1)
                                .to_broadcast([KCS, KC, NKV, HD]), ALU.add).then_inc(v_ready[O], 1)
                        if a_ok:
                            if k == 2:
                                need(dve, mask_in[O], 16 * (ahead + 1))
                            for hh in range(HEAD0[k], HEAD0[k + 1]):
                                maximum(hh)
                        if k in (3, 4) and p_ok:
                            c0 = (k - 3) * GL // 2
                            if k == 3:
                                need(dve, o_in[O], 64 * (post + 1))
                            nc.vector.reciprocal(orec[:, c0:c0 + GL // 2], osum[:, c0:c0 + GL // 2])\
                              .then_inc(o_rec[O], 1)
                        if k == 4 and p_ok:
                            need(dve, o_rec[O], 2 * (post + 1))
                            nc.vector.tensor_tensor(on[:, :], oc[:, :], orec[:, :], ALU.mult)\
                              .then_inc(on_ready[O], 1)
                        if k == 6 and p_ok:
                            need(dve, o_ps[O], post + 1)
                            need(dve, res_ready[O], post + 1)
                            nc.vector.tensor_tensor(tsum[:, :], job[0:S, 0:D], res[O][:, :], ALU.add)\
                              .then_inc(o_evac[O], 1)
                            need(dve, o_evac[O], post + 1)
                            nc.vector.bn_stats(stats[:, :], tsum[:, :]).then_inc(ln[O], 1)
                            need(dve, ln[O], 3 * post + 1)
                            nc.vector.memset(pause[:, :], 0.0)
                            nc.vector.bn_aggr(mv[:, :], stats[:, :]).then_inc(ln[O], 1)
                            need(dve, ln[O], 3 * post + 2)
                            nc.vector.tensor_scalar(veps[:, :], mv[:, 1:2], EPS, None, ALU.add).then_inc(ln[O], 1)
                        if k == 7:
                            if a_ok:
                                max_parts(O, 0, ahead)
                            if p_ok:
                                need(dve, rs_ready[O], post + 1)
                                nc.vector.tensor_scalar(z[:, :], tsum[:, :], mv[:, 0:1], rstd[:, 0:1], ALU.subtract,
                                                        ALU.mult).then_inc(z_ready[O], 1)
                return slot

            dve.wait_ge(flag_ok, 2)
            any_mask = dve.value_load(mflag[0:1, 0:1], min_val=0, max_val=1)
            with dve.If(any_mask == 0):
                run(dve, slots(False))
            with dve.Else():
                run(dve, slots(True))

        @block.tensor
        def _(pe):
            def slots(masked):
                def slot(L, i, has):
                    main, ahead, post, proj = units(L, i)
                    m_ok, a_ok, p_ok, j_ok = has
                    O = 1 - L
                    job_free = [(q_evac[O], NG * (ahead + 1)) if a_ok else (mt_evac[L], 2 * main + 1) if m_ok else None]

                    def take_job_bank():
                        if job_free[0] is not None:
                            need(pe, *job_free[0])

                    def scores(k):
                        chunk, groups = piece(k)
                        if k == 0 or k == HALF:
                            need(pe, m_rows[L][k // HALF], 16 * (main + 1))
                        if k >= 2:
                            need(pe, exp_done[L], PIECES * main + k - 1)
                        elif p_ok:
                            need(pe, exp_done[O], PIECES * post + PIECES - 1 + k)
                        rows = slice(KCS * chunk, KCS * chunk + KCS)
                        for j, g in enumerate(groups):
                            last = nc.tensor.matmul(sc[k % 2][0:KCS, j, 0:GL], ks[L][0:KM, g, rows], qs[L][0:KM, g, :],
                                                    start=True, stop=not masked)
                            if masked:
                                last = nc.tensor.matmul(sc[k % 2][0:KCS, j, 0:GL], mask[L][:, rows],
                                                        ident4[:, :, :].rearrange("p c l -> p (c l)"),
                                                        start=False, stop=True)
                        last.then_inc(sc_ps[L], 1)

                    def maximum(hh):
                        if hh % HH == 0:
                            need(pe, stack[O][hh // HH], 16 * NSTACK * (ahead + 1))
                        if hh >= 2:
                            need(pe, max_done[O], NH * ahead + hh - 1)
                        elif m_ok:
                            need(pe, max_done[L], NH * main + NH - 1 + hh)
                        g, c = hh // NG, hh % NG
                        nc.tensor.matmul(ms[hh % 2][0:S, 0:S2], qs[O][0:KT, g, S * c:S * c + S], ks[O][0:KT, g, :],
                                         start=True, stop=True).then_inc(ms_ps[O], 1)

                    def values(U, q, b, before):
                        half, chunk = q // KC, q % KC
                        need(pe, exp_done[U], PIECES * b + 2 * q + 2)
                        if q == 0:
                            need(pe, v_ready[U], b + 1)
                            if before is not None:
                                need(pe, pv_evac[before[0]][1], before[1] + 1)
                        if q == KC:
                            need(pe, pv_evac[U][0], b + 1)
                        for j in range(4):
                            last = nc.tensor.matmul(pv[32 * j:32 * j + 32, 0:GL], vs[U][:, chunk, 4 * half + j, :, :].rearrange("s d two -> s (d two)"),
                                                    probs[:, (2 * q + j // 2) % RING, j % 2, :],
                                                    start=(chunk == 0), stop=(chunk == KC - 1))
                        last.then_inc(pv_ps[U], 1)

                    def max_columns(U, h, b):
                        take_job_bank()
                        need(pe, m_part[U], 4 * (2 * b + h + 1))
                        nc.tensor.transpose(jobb[0:2 * PARTS * HH, 0:S], mp[:, :, :].rearrange("p a b -> p (a b)"),
                                            identb[:, :]).then_inc(mt_ps[U], 1)
                        job_free[0] = (mt_evac[U], 2 * b + h + 1)

                    def project_values():
                        take_job_bank()
                        need(pe, ctx_in[O], 16 * (ahead + 1))
                        for c in range(KC):
                            for t in range(DC):
                                last = nc.tensor.matmul(job[0:KCS, P * c:P * c + P], ctxT[O][:, t, KCS * c:KCS * c + KCS],
                                                        wv[O][:, t, :], start=(t == 0), stop=(t == DC - 1))
                        last.then_inc(v_ps[O], 1)
                        job_free[0] = (v_ready[O], ahead + 1)

                    def project_keys():
                        take_job_bank()
                        need(pe, ctx_in[L], 16 * (proj + 1))
                        for t in range(DC):
                            last = nc.tensor.matmul(job[:, 0:S2], wk[L][:, t, :], ctxT[L][:, t, :],
                                                    start=(t == 0), stop=(t == DC - 1))
                        last.then_inc(k_ps[L], 1)
                        job_free[0] = (k_evac[L], proj + 1)

                    def project_outputs():
                        take_job_bank()
                        need(pe, on_ready[O], post + 1)
                        for c in range(NG):
                            last = nc.tensor.matmul(job[0:S, 0:D], on[:, S * c:S * c + S], wo[O][:, c, :],
                                                    start=(c == 0), stop=(c == NG - 1))
                        last.then_inc(o_ps[O], 1)
                        job_free[0] = (o_evac[O], post + 1)

                    def transpose_rows():
                        take_job_bank()
                        need(pe, y_ready[0], post + 1)
                        for t in range(DC):
                            last = nc.tensor.transpose(job[:, S * t:S * t + S], y[0][:, P * t:P * t + P], ident[0:S, 0:S])
                        last.then_inc(t_ps, 1)
                        job_free[0] = (xT_ready, post + 1)

                    def project_queries(c0):
                        if c0 == 0:
                            take_job_bank()
                            if L == 0:
                                need(pe, xT_in, 16 * (proj + 1))
                            else:
                                need(pe, xT_ready, proj + 1)
                        for c in (c0, c0 + 1):
                            for t in range(DC):
                                last = nc.tensor.matmul(job[:, S * c:S * c + S], wq[L][:, t, c, :], xT[L][:, t, :],
                                                        start=(t == 0), stop=(t == DC - 1))
                        if c0:
                            last.then_inc(q_ps[L], 1)

                    for k in range(PIECES):
                        if m_ok:
                            scores(k)
                        if k == 0 and p_ok:
                            values(O, NPV - 1, post, None)
                        if k == 1 and m_ok:
                            max_columns(L, 1, main)
                        if k == 2 and a_ok:
                            project_values()
                        if k == 3 and j_ok:
                            project_keys()
                        if a_ok:
                            for hh in range(HEAD0[k], HEAD0[k + 1]):
                                maximum(hh)
                        if k == 5 and p_ok:
                            project_outputs()
                        if k == 7 and a_ok:
                            max_columns(O, 0, ahead)
                        if k == 8 and p_ok and O == 0:
                            transpose_rows()
                        if k == 9 and j_ok:
                            project_queries(0)
                        if k == 10 and j_ok:
                            project_queries(2)
                        if k >= 2 and k % 2 == 0 and m_ok:
                            values(L, (k - 2) // 2, main, (O, post) if p_ok else None)
                return slot

            pe.wait_ge(idd, 3)
            pe.wait_ge(w_in, 16 * NW)
            pe.wait_ge(flag_col, 1)
            nc.tensor.transpose(job[0:1, 0:P], mcol[:, :], ident[:, :]).then_inc(flag_row, 1)
            pe.wait_ge(flag_ok, 2)
            any_mask = pe.value_load(mflag[0:1, 0:1], min_val=0, max_val=1)
            with pe.If(any_mask == 0):
                run(pe, slots(False))
            with pe.Else():
                run(pe, slots(True))


def run(eng, slot):
    FIRST, STEADY, LAST = -1, 3, B - 2
    for i in range(FIRST, STEADY):
        for L in range(LAYERS):
            slot(L, i, exists(L, i))
    with eng.Fori(STEADY, LAST) as i:
        for L in range(LAYERS):
            slot(L, i, exists(L, None))
    for i in range(LAST, B + 2):
        for L in range(LAYERS):
            slot(L, i, exists(L, i))


def kernel(**inputs):
    import numpy as np
    import concourse.bacc as bacc
    from concourse.bass_utils import run_bass_kernel_spmd

    nc = bacc.Bacc("TRN2", target_bir_lowering=False, num_devices=1)
    arrays = {}

    def put(name, a):
        a = np.ascontiguousarray(a)
        arrays["in_" + name] = a
        return nc.dram_tensor("in_" + name, a.shape, mybir.dt.from_np(a.dtype), kind="ExternalInput").ap()

    x = np.asarray(inputs["x"])
    c = np.asarray(inputs["ctx_2048"])
    m = np.asarray(inputs["mask_Bx1xSxS2_ff0"])
    xT_d = put("xT", x.reshape(B, S, DC, P).transpose(0, 3, 2, 1).reshape(B, P, DC * S))
    x_d = put("x", x)
    ctxT_d = put("ctxT", c.reshape(B, S2, DC, P).transpose(0, 3, 2, 1).reshape(B, P, DC * S2))
    mask_d = put("mask", m.reshape(B, S, S2))
    mflat_d = put("mask_bits", m.reshape(P, B * S * S2 // P).view(np.uint32))
    W = []
    for L in range(LAYERS):
        w = {k: np.asarray(inputs[f"L{L}_xattn_{k}"])
             for k in ("Wq", "bq", "Wk", "bk", "Wv", "bv", "Wo", "bo", "gamma", "beta")}
        W.append({
            "Wq": put(f"Wq{L}", w["Wq"].reshape(DC, P, 2, 4, NG, HD).transpose(1, 0, 4, 2, 5, 3).reshape(P, DC * D)),
            "Wk": put(f"Wk{L}", w["Wk"].reshape(DC, P, 2, 4, HD).transpose(1, 0, 2, 4, 3).reshape(P, DC * P)),
            "Wv": put(f"Wv{L}", w["Wv"].reshape(DC, P, P).transpose(1, 0, 2).reshape(P, DC * P)),
            "Wo": put(f"Wo{L}", w["Wo"].reshape(NKV, NG, HD, D).transpose(0, 2, 1, 3).reshape(P, NG * D)),
            "bq": put(f"bq{L}", w["bq"].reshape(2, 4, NG, HD).transpose(0, 3, 1, 2).reshape(P, NG)),
            "bk": put(f"bk{L}", w["bk"].reshape(2, 4, HD).transpose(0, 2, 1).reshape(P, 1)),
            "bv": put(f"bv{L}", w["bv"].reshape(1, P)),
            "bo": put(f"bo{L}", w["bo"].reshape(1, D)),
            "gamma": put(f"gamma{L}", w["gamma"].reshape(1, D)),
            "beta": put(f"beta{L}", w["beta"].reshape(1, D)),
        })
    out = nc.dram_tensor("out", (B, S, D), F32, kind="ExternalOutput").ap()
    cross_attention_two_layers(nc, xT_d, x_d, ctxT_d, mask_d, mflat_d, W, out)
    r = run_bass_kernel_spmd(nc, [arrays], core_ids=[0])
    return r.results[0]["out"]
```

```python
import concourse.bass as bass
from concourse import mybir
from contextlib import ExitStack

F32 = mybir.dt.float32
BF16 = mybir.dt.bfloat16
U32 = mybir.dt.uint32
I32 = mybir.dt.int32
ALU = mybir.AluOpType
ACT = mybir.ActivationFunctionType
AX_X = mybir.AxisListType.X

B, S, S2, D = 32, 112, 375, 512
NH, NKV, HD = 32, 8, 16
NG = NH // NKV
LAYERS = 2
P = 128
DC = D // P
KC = 3
KCS = S2 // KC
GL = NG * S
SCALE = float(HD) ** -0.5
EPS = 1e-6
LOWEST = -3.0e38

TERMS = [(0, 0), (0, 1), (1, 0), (1, 1), (0, 2), (2, 0)]
NT = len(TERMS)
KT = NT * HD
PARTS = 3
KM = KT + PARTS

MLOADS = 2
MROW = B * S * S2 // (MLOADS * KCS)

PIECES = 12
HALF = PIECES // 2
NPV = PIECES // 2
RING = 6
HEADS_AT = [0, 0, 0, 2, 3, 4, 3, 4, 5, 4, 4, 3]
HEAD0 = [sum(HEADS_AT[:k]) for k in range(PIECES + 1)]
HH = NH // 2
NSTACK = 2 * NT
assert KCS * KC == S2 and HEAD0[-1] == NH and KM <= P and HEAD0[8] == HH


def units(L, i):
    main = i if L == 0 else i - 1
    ahead = i - 1 if L == 0 else i + 1
    post = ahead - 1
    proj = main + 1
    return main, ahead, post, proj


def exists(L, i):
    if i is None:
        return True, True, True, True
    return tuple(0 <= b < B for b in units(L, i))


def need(eng, sem, value):
    if isinstance(value, int) and value <= 0:
        return
    eng.wait_ge(sem, value)


def piece(k):
    half, chunk, pair = k // HALF, (k % HALF) // 2, k % 2
    return chunk, [4 * half + 2 * pair + j for j in range(2)]


def cross_attention_two_layers(nc, xT_d, x_d, ctxT_d, mask_d, mflat_d, W, out):
    with ExitStack() as ctx:
        def sb(name, shape, dt=F32):
            return ctx.enter_context(nc.sbuf_tensor(name, shape, dt))

        def ps(name, shape, dt=F32):
            return ctx.enter_context(nc.psum_tensor(name, shape, dt))

        def sem(name):
            return ctx.enter_context(nc.semaphore(name))

        def per_layer(make, name, *a):
            return [make(f"{name}{L}", *a) for L in range(LAYERS)]

        wq = per_layer(sb, "wq", [P, DC, NG, P])
        wk = per_layer(sb, "wk", [P, DC, P])
        wv = per_layer(sb, "wv", [P, DC, P])
        wo = per_layer(sb, "wo", [P, NG, D])
        bq = per_layer(sb, "bq", [P, NG])
        bqs = per_layer(sb, "bqs", [P, NG])
        bk = per_layer(sb, "bk", [P, 1])
        bv = per_layer(sb, "bv", [KCS, P])
        bo = per_layer(sb, "bo", [S, D])
        gamma = per_layer(sb, "gamma", [S, D])
        beta = per_layer(sb, "beta", [S, D])
        ident = sb("ident", [P, P])
        ident4 = sb("ident4", [S, NG, S])
        identb = sb("identb", [S, S], BF16)
        neghalf = sb("neghalf", [S, 1])
        pause = sb("pause", [S, 1])
        mcols = sb("mcols", [KCS, MLOADS])
        mcol = sb("mcol", [KCS, 1])
        mrow = sb("mrow", [1, 2])
        mflag = sb("mflag", [1, 1], I32)
        ctxT = per_layer(sb, "ctxT", [P, DC, S2])
        xT = per_layer(sb, "xT", [P, DC, S])
        xin = sb("xin", [S, D])
        mask = per_layer(sb, "mask", [S, S2])
        qf = sb("qf", [P, GL])
        qr = sb("qr", [P, GL])
        qp = sb("qp", [P, PARTS, GL], BF16)
        kf = sb("kf", [P, S2])
        kr = sb("kr", [P, S2])
        kp = sb("kp", [P, PARTS, S2], BF16)
        qs = per_layer(sb, "qs", [P, NKV, GL], BF16)
        ks = per_layer(sb, "ks", [P, NKV, S2], BF16)
        vs = per_layer(sb, "vs", [KCS, KC, NKV, HD, 2])
        scratch = sb("scratch", [S, S2])
        mx = per_layer(sb, "mx", [S, NH])
        mr = sb("mr", [S, HH])
        mp = sb("mp", [S, 2 * PARTS, HH], BF16)
        mT = sb("mT", [PARTS * HH, S], BF16)
        probs = sb("probs", [KCS, RING, 2, GL])
        mbits = probs[:, :, :, :].rearrange("p a b c -> p (a b c)").bitcast(U32)[:, 0:MROW]
        oraw = [sb(f"oraw{h}", [P, GL]) for h in range(2)]
        oc = sb("oc", [P, GL])
        osum = sb("osum", [P, GL])
        orec = sb("orec", [P, GL])
        on = sb("on", [P, GL])
        res = per_layer(sb, "res", [S, D])
        tsum = sb("tsum", [S, D])
        stats = sb("stats", [S, 6])
        mv = sb("mv", [S, 2])
        veps = sb("veps", [S, 1])
        rstd = sb("rstd", [S, 1])
        zg = sb("zg", [S, D])
        y = per_layer(sb, "y", [S, D])

        sc = [ps(f"sc{h}", [P, 2, 512]) for h in range(2)]
        ms = [ps(f"ms{h}", [P, 512]) for h in range(2)]
        pv = ps("pv", [P, 512])
        job = ps("job", [P, 512])
        jobb = job[:, :].bitcast(BF16)

        w_in = sem("w_in")
        mf_in = sem("mf_in")
        consts = sem("consts")
        ids = sem("ids")
        idd = sem("idd")
        flag_col = sem("flag_col")
        flag_row = sem("flag_row")
        flag_ok = sem("flag_ok")
        ctx_in = per_layer(sem, "ctx_in")
        mask_in = per_layer(sem, "mask_in")
        xT_in = sem("xT_in")
        x_in = sem("x_in")
        k_ps = per_layer(sem, "k_ps")
        v_ps = per_layer(sem, "v_ps")
        q_ps = per_layer(sem, "q_ps")
        o_ps = per_layer(sem, "o_ps")
        t_ps = sem("t_ps")
        mt_ps = per_layer(sem, "mt_ps")
        k_evac = per_layer(sem, "k_evac")
        q_evac = per_layer(sem, "q_evac")
        k_p1 = per_layer(sem, "k_p1")
        k_r = per_layer(sem, "k_r")
        k_p2 = per_layer(sem, "k_p2")
        k_p3 = per_layer(sem, "k_p3")
        q_p1 = per_layer(sem, "q_p1")
        q_r = per_layer(sem, "q_r")
        q_p2 = per_layer(sem, "q_p2")
        q_p3 = per_layer(sem, "q_p3")
        v_ready = per_layer(sem, "v_ready")
        xT_ready = sem("xT_ready")
        stack = [[sem(f"stack{L}{h}") for h in range(2)] for L in range(LAYERS)]
        m_rows = [[sem(f"m_rows{L}{h}") for h in range(2)] for L in range(LAYERS)]
        ms_ps = per_layer(sem, "ms_ps")
        m_masked = per_layer(sem, "m_masked")
        max_done = per_layer(sem, "max_done")
        m_part = per_layer(sem, "m_part")
        mt_evac = per_layer(sem, "mt_evac")
        sc_ps = per_layer(sem, "sc_ps")
        exp_done = per_layer(sem, "exp_done")
        pv_ps = per_layer(sem, "pv_ps")
        pv_evac = [[sem(f"pv_evac{L}{h}") for h in range(2)] for L in range(LAYERS)]
        o_in = per_layer(sem, "o_in")
        o_rec = per_layer(sem, "o_rec")
        on_ready = per_layer(sem, "on_ready")
        res_ready = per_layer(sem, "res_ready")
        o_evac = per_layer(sem, "o_evac")
        ln = per_layer(sem, "ln")
        rs_ready = per_layer(sem, "rs_ready")
        zg_ready = per_layer(sem, "zg_ready")
        y_ready = per_layer(sem, "y_ready")
        out_done = sem("out_done")

        NW = 10 * LAYERS
        block = ctx.enter_context(nc.Block())

        @block.sync
        def _(sp):
            def load_ctx(L, b):
                sp.dma_start(ctxT[L][:, :, :].rearrange("p a b -> p (a b)"), ctxT_d[b]).then_inc(ctx_in[L], 16)

            def load_mask(L, b):
                sp.dma_start(mask[L][:, :], mask_d[b]).then_inc(mask_in[L], 16)

            def load_xT(b):
                sp.dma_start(xT[0][:, :, :].rearrange("p a b -> p (a b)"), xT_d[b]).then_inc(xT_in, 16)

            def load_x(b):
                sp.dma_start(xin[:, :], x_d[b]).then_inc(x_in, 16)

            def stack_terms(L, h, dst, src, which, of=range(PARTS)):
                for t, parts in enumerate(TERMS):
                    if parts[which] not in of:
                        continue
                    sp.dma_start(dst[HD * t:HD * t + HD, 4 * h:4 * h + 4, :].rearrange("d g n -> d (g n)"),
                                 src[64 * h:64 * h + 64, parts[which], :]).then_inc(stack[L][h], 16)

            def max_rows(L, h, count):
                need(sp, mt_evac[L], count)
                sp.dma_start(qs[L][KT:KM, 4 * h:4 * h + 4, :].rearrange("p g n -> p (g n)"), mT[:, :])\
                  .then_inc(m_rows[L][h], 16)

            def outputs(L, h, count):
                need(sp, pv_evac[L][h], count)
                for dst, r0 in ((oc, 0), (osum, 1)):
                    sp.dma_start(dst[64 * h:64 * h + 64, :], oraw[h][r0::2, :]).then_inc(o_in[L], 16)

            def slot(L, i, has):
                main, ahead, post, proj = units(L, i)
                m_ok, a_ok, p_ok, j_ok = has
                O = 1 - L

                def count(value):
                    return value if isinstance(value, int) else sp.snap(value)

                mains, projs, aheads = count(main), count(proj), count(ahead)
                projs1, aheads1 = count(proj + 1), count(ahead + 1)
                main_half2 = count(2 * main + 2)
                ahead_half1 = count(2 * ahead + 1)
                post_scores = count(PIECES * ahead)
                if a_ok:
                    need(sp, sc_ps[O], post_scores)
                    load_mask(O, aheads)
                if p_ok:
                    outputs(O, 1, aheads)
                if a_ok:
                    need(sp, q_p3[O], aheads1)
                    stack_terms(O, 0, qs[O], qp, 0, of=(2,))
                if m_ok:
                    max_rows(L, 1, main_half2)
                if a_ok:
                    stack_terms(O, 1, ks[O], kp, 1)
                    stack_terms(O, 1, qs[O], qp, 0)
                if L == 0 and j_ok:
                    need(sp, q_ps[0], projs)
                    load_xT(projs)
                if L == 0 and m_ok:
                    need(sp, res_ready[0], mains)
                    load_x(mains)
                if a_ok and not (isinstance(ahead, int) and ahead + 1 >= B):
                    need(sp, v_ps[O], aheads1)
                    load_ctx(O, aheads1)
                if m_ok:
                    if p_ok:
                        need(sp, on_ready[O], aheads)
                    outputs(L, 0, projs)
                if a_ok:
                    max_rows(O, 0, ahead_half1)
                if p_ok and O == 1:
                    need(sp, y_ready[1], aheads)
                    sp.dma_start(out[post], y[1][:, :]).then_inc(out_done, 16)
                if j_ok:
                    need(sp, k_p3[L], projs1)
                    stack_terms(L, 0, ks[L], kp, 1)
                    need(sp, q_p1[L], projs1)
                    stack_terms(L, 0, qs[L], qp, 0, of=(0,))
                    need(sp, q_p2[L], projs1)
                    stack_terms(L, 0, qs[L], qp, 0, of=(1,))

            def load_rows(L):
                for dst, key in ((bv, "bv"), (bo, "bo"), (gamma, "gamma"), (beta, "beta")):
                    n = dst[L].shape[0]
                    sp.dma_start(dst[L][:, :], W[L][key].to_broadcast([n, dst[L].shape[1]])).then_inc(w_in, 16)

            for L in range(LAYERS):
                sp.dma_start(wk[L][:, :, :].rearrange("p a b -> p (a b)"), W[L]["Wk"]).then_inc(w_in, 16)
                load_ctx(L, 0)
                sp.dma_start(wq[L][:, :, :, :].rearrange("p a b c -> p (a b c)"), W[L]["Wq"]).then_inc(w_in, 16)
                sp.dma_start(wv[L][:, :, :].rearrange("p a b -> p (a b)"), W[L]["Wv"]).then_inc(w_in, 16)
                sp.dma_start(wo[L][:, :, :].rearrange("p a b -> p (a b)"), W[L]["Wo"]).then_inc(w_in, 16)
                sp.dma_start(bq[L][:, :], W[L]["bq"]).then_inc(w_in, 16)
                sp.dma_start(bk[L][:, :], W[L]["bk"]).then_inc(w_in, 16)
                load_rows(L)
            for n in range(MLOADS):
                need(sp, flag_col, n)
                sp.dma_start(mbits, mflat_d[n]).then_inc(mf_in, 16)
            sp.wait_ge(consts, 1)
            run(sp, slot)
            sp.wait_ge(out_done, 16 * B)

        @block.gpsimd
        def _(pool):
            nc.gpsimd.memset(ident[:, :], 0.0).then_inc(ids, 1)
            nc.gpsimd.memset(ident4[:, :, :], 0.0).then_inc(ids, 1)
            nc.gpsimd.memset(neghalf[:, :], -0.5).then_inc(ids, 1)
            pool.wait_ge(ids, 3)
            nc.gpsimd.affine_select(out=ident[:, :], in_=ident[:, :], compare_op=ALU.not_equal, fill=1.0,
                                    base=0, pattern=[[-1, P]], channel_multiplier=1).then_inc(idd, 1)
            nc.gpsimd.affine_select(out=ident4[:, :, :], in_=ident4[:, :, :], compare_op=ALU.not_equal, fill=1.0,
                                    base=0, pattern=[[0, NG], [-1, S]], channel_multiplier=1).then_inc(idd, 1)

            def slot(L, i, has):
                main, ahead, post, proj = units(L, i)
                m_ok, a_ok, p_ok, j_ok = has
                O = 1 - L
                if p_ok and O == 0:
                    need(pool, x_in, 16 * (post + 1))
                    need(pool, o_evac[0], post)
                    nc.gpsimd.tensor_tensor(res[0][:, :], xin[:, :], bo[0][:, :], ALU.add).then_inc(res_ready[0], 1)
                if p_ok:
                    need(pool, ln[O], 3 * (post + 1))
                    nc.gpsimd.tensor_tensor(rstd[:, :], veps[:, :], neghalf[:, :], ALU.pow).then_inc(rs_ready[O], 1)
                if j_ok:
                    need(pool, k_p1[L], proj + 1)
                    nc.gpsimd.tensor_tensor(kr[:, :], kf[:, :], kp[:, 0, :], ALU.subtract).then_inc(k_r[L], 1)
                    need(pool, k_p2[L], proj + 1)
                    nc.gpsimd.tensor_tensor(kp[:, 2, :], kr[:, :], kp[:, 1, :], ALU.subtract).then_inc(k_p3[L], 1)
                if a_ok and O == 1:
                    need(pool, y_ready[0], ahead + 1)
                    need(pool, o_evac[1], ahead)
                    nc.gpsimd.tensor_tensor(res[1][:, :], y[0][:, :], bo[1][:, :], ALU.add).then_inc(res_ready[1], 1)
                if j_ok:
                    need(pool, q_p1[L], proj + 1)
                    nc.gpsimd.tensor_tensor(qr[:, :], qf[:, :], qp[:, 0, :], ALU.subtract).then_inc(q_r[L], 1)
                    need(pool, q_p2[L], proj + 1)
                    nc.gpsimd.tensor_tensor(qp[:, 2, :], qr[:, :], qp[:, 1, :], ALU.subtract).then_inc(q_p3[L], 1)

            pool.wait_ge(w_in, 16 * NW)
            run(pool, slot)

        @block.scalar
        def _(act):
            def slot(L, i, has):
                main, ahead, post, proj = units(L, i)
                m_ok, a_ok, p_ok, j_ok = has
                O = 1 - L

                def exp(k):
                    if not m_ok:
                        return
                    need(act, sc_ps[L], PIECES * main + k + 1)
                    if k >= RING:
                        need(act, pv_ps[L], NPV * main + (k - RING) // 2 + 1)
                    elif p_ok:
                        need(act, pv_ps[O], NPV * post + (PIECES - RING + k) // 2 + 1)
                    nc.scalar.activation(probs[:, k % RING, :, :], sc[k % 2][0:KCS, :, 0:GL], ACT.Exp)\
                      .then_inc(exp_done[L], 1)

                def pv_out(U, h, b, before):
                    need(act, pv_ps[U], NPV * b + 3 * (h + 1))
                    if before is not None:
                        need(act, o_in[before[0]], 64 * before[1] + 32 * (h + 1))
                    nc.scalar.copy(oraw[h][:, :], pv[:, 0:GL]).then_inc(pv_evac[U][h], 1)

                def m_out(U, h, b, rows):
                    need(act, mt_ps[U], 2 * b + h + 1)
                    if rows is not None:
                        need(act, m_rows[rows[0]][1 - h], 16 * rows[1])
                    nc.scalar.copy(mT[:, :], jobb[0:PARTS * HH, 0:S]).then_inc(mt_evac[U], 1)

                for k in range(PIECES):
                    if k == 9 and p_ok and O == 0:
                        need(act, t_ps, post + 1)
                        need(act, q_ps[1], post)
                        nc.scalar.copy(xT[1][:, :, :].rearrange("p a b -> p (a b)"), job[:, 0:GL])\
                          .then_inc(xT_ready, 1)
                    exp(k)
                    if k == 0 and m_ok:
                        m_out(L, 1, main, (L, main + 1))
                    if k == 0 and p_ok:
                        first, last = isinstance(main, int) and main < 1, isinstance(main, int) and main > B
                        pv_out(O, 1, post, (O, post - 1) if last else None if first else (L, main - 1))
                    if k == 7 and j_ok:
                        need(act, k_ps[L], proj + 1)
                        if a_ok:
                            need(act, k_r[O], ahead + 1)
                            need(act, stack[O][0], 16 * NSTACK * (ahead + 1))
                            need(act, stack[O][1], 16 * NSTACK * (ahead + 1))
                        nc.scalar.activation(kf[:, :], job[:, 0:S2], ACT.Identity, bias=bk[L][:, 0:1])\
                          .then_inc(k_evac[L], 1)
                        need(act, k_evac[L], proj + 1)
                        nc.scalar.copy(kp[:, 0, :], kf[:, :]).then_inc(k_p1[L], 1)
                    if k == 8 and j_ok:
                        need(act, k_r[L], proj + 1)
                        nc.scalar.copy(kp[:, 1, :], kr[:, :]).then_inc(k_p2[L], 1)
                    if k == 7 and m_ok:
                        pv_out(L, 0, main, (O, post) if p_ok else None)
                    if k == 8 and a_ok:
                        m_out(O, 0, ahead, (L, main + 1) if m_ok else None)
                    if k == 10 and j_ok:
                        need(act, q_ps[L], proj + 1)
                        if a_ok:
                            need(act, q_r[O], ahead + 1)
                        for c in range(NG):
                            nc.scalar.activation(qf[:, S * c:S * c + S], job[:, S * c:S * c + S], ACT.Identity,
                                                 bias=bqs[L][:, c:c + 1], scale=SCALE).then_inc(q_evac[L], 1)
                        need(act, q_evac[L], NG * (proj + 1))
                        nc.scalar.copy(qp[:, 0, :], qf[:, :]).then_inc(q_p1[L], 1)
                    if k == 11 and j_ok:
                        need(act, q_r[L], proj + 1)
                        nc.scalar.copy(qp[:, 1, :], qr[:, :]).then_inc(q_p2[L], 1)

            act.wait_ge(w_in, 16 * NW)
            act.wait_ge(consts, 1 + LAYERS)
            run(act, slot)

        @block.vector
        def _(dve):
            for L in range(LAYERS):
                nc.vector.memset(qs[L][:, :, :].bitcast(U32), 0)
                nc.vector.memset(ks[L][:, :, :], 1.0)
                nc.vector.memset(vs[L][:, :, :, :, 1], 1.0)
            last = nc.vector.memset(mp[:, :, :], 0.0)
            last.then_inc(consts, 1)
            dve.wait_ge(w_in, 16 * NW)
            for L in range(LAYERS):
                nc.vector.tensor_scalar(bqs[L][:, :], bq[L][:, :], SCALE, None, ALU.mult).then_inc(consts, 1)
            dve.wait_ge(idd, 2)
            nc.vector.tensor_copy(identb[:, :], ident[0:S, 0:S]).then_inc(idd, 1)
            for n in range(MLOADS):
                dve.wait_ge(mf_in, 16 * (n + 1))
                nc.vector.tensor_reduce(mcols[:, n:n + 1], mbits, AX_X, ALU.max).then_inc(flag_col, 1)
            dve.wait_ge(flag_col, MLOADS)
            nc.vector.tensor_reduce(mcol[:, :], mcols[:, :], AX_X, ALU.max).then_inc(flag_col, 1)
            dve.wait_ge(flag_row, 1)
            nc.vector.tensor_reduce(mrow[:, 0:1], job[0:1, 0:KCS], AX_X, ALU.max).then_inc(flag_ok, 1)
            dve.wait_ge(flag_ok, 1)
            nc.vector.tensor_scalar(mflag[:, :], mrow[:, 0:1], 0.0, None, ALU.is_gt).then_inc(flag_ok, 1)

            def slots(masked):
                def slot(L, i, has):
                    main, ahead, post, proj = units(L, i)
                    m_ok, a_ok, p_ok, j_ok = has
                    O = 1 - L

                    def maximum(hh):
                        need(dve, ms_ps[O], NH * ahead + hh + 1)
                        if masked:
                            nc.vector.tensor_tensor(scratch[:, :], ms[hh % 2][0:S, 0:S2], mask[O][:, :], ALU.add)\
                              .then_inc(m_masked[O], 1)
                            need(dve, m_masked[O], NH * ahead + hh + 1)
                            nc.vector.tensor_reduce(mx[O][:, hh:hh + 1], scratch[:, :], AX_X, ALU.max)\
                              .then_inc(max_done[O], 1)
                            need(dve, max_done[O], NH * ahead + hh + 1)
                        else:
                            nc.vector.tensor_reduce(mx[O][:, hh:hh + 1], ms[hh % 2][0:S, 0:S2], AX_X, ALU.max)\
                              .then_inc(max_done[O], 1)

                    def max_parts(U, h, b):
                        cols = mx[U][:, HH * h:HH * h + HH]
                        done = 4 * (2 * b + h)
                        need(dve, max_done[U], NH * b + HH * (h + 1))
                        if h == 1:
                            need(dve, mt_ps[U], 2 * b + 1)
                        elif m_ok:
                            need(dve, mt_ps[L], 2 * main + 2)
                        nc.vector.tensor_scalar(mp[:, 0, :], cols, -1.0, None, ALU.mult).then_inc(m_part[U], 1)
                        need(dve, m_part[U], done + 1)
                        nc.vector.scalar_tensor_tensor(out=mr[:, :], in0=cols, scalar=-1.0, in1=mp[:, 0, :],
                                                       op0=ALU.mult, op1=ALU.subtract).then_inc(m_part[U], 1)
                        need(dve, m_part[U], done + 2)
                        nc.vector.tensor_copy(mp[:, 1, :], mr[:, :]).then_inc(m_part[U], 1)
                        need(dve, m_part[U], done + 3)
                        nc.vector.tensor_tensor(mp[:, 2, :], mr[:, :], mp[:, 1, :], ALU.subtract)\
                          .then_inc(m_part[U], 1)

                    if m_ok:
                        max_parts(L, 1, main)
                    for k in range(PIECES):
                        if k == 3 and a_ok:
                            need(dve, v_ps[O], ahead + 1)
                            if p_ok:
                                need(dve, pv_ps[O], NPV * (post + 1))
                            nc.vector.tensor_tensor(
                                vs[O][:, :, :, :, 0], job[0:KCS, 0:KC * P].rearrange("p (c g d) -> p c g d", c=KC, d=HD),
                                bv[O][:, :].rearrange("p (g d) -> p g d", d=HD).unsqueeze(1)
                                .to_broadcast([KCS, KC, NKV, HD]), ALU.add).then_inc(v_ready[O], 1)
                        if k == 6 and p_ok:
                            need(dve, o_ps[O], post + 1)
                            need(dve, res_ready[O], post + 1)
                            nc.vector.tensor_tensor(tsum[:, :], job[0:S, 0:D], res[O][:, :], ALU.add)\
                              .then_inc(o_evac[O], 1)
                        if k == 8 and a_ok:
                            max_parts(O, 0, ahead)
                        if k == 7 and p_ok:
                            need(dve, rs_ready[O], post + 1)
                            need(dve, zg_ready[O], post + 1)
                            if O == 1:
                                need(dve, out_done, 16 * post)
                            else:
                                need(dve, t_ps, post)
                                need(dve, res_ready[1], post)
                            nc.vector.scalar_tensor_tensor(out=y[O][:, :], in0=zg[:, :], scalar=rstd[:, 0:1], in1=beta[O][:, :],
                                                           op0=ALU.mult, op1=ALU.add).then_inc(y_ready[O], 1)
                        if a_ok:
                            if k == 3:
                                need(dve, mask_in[O], 16 * (ahead + 1))
                            for hh in range(HEAD0[k], HEAD0[k + 1]):
                                maximum(hh)
                        if k == 2 and p_ok:
                            need(dve, o_in[O], 64 * (post + 1))
                            nc.vector.reciprocal(orec[:, :], osum[:, :]).then_inc(o_rec[O], 1)
                            need(dve, o_rec[O], post + 1)
                            nc.vector.tensor_tensor(on[:, :], oc[:, :], orec[:, :], ALU.mult)\
                              .then_inc(on_ready[O], 1)
                        if k == 6 and p_ok:
                            need(dve, o_evac[O], post + 1)
                            nc.vector.bn_stats(stats[:, :], tsum[:, :]).then_inc(ln[O], 1)
                            need(dve, ln[O], 3 * post + 1)
                            nc.vector.memset(pause[:, :], 0.0)
                            nc.vector.bn_aggr(mv[:, :], stats[:, :]).then_inc(ln[O], 1)
                            need(dve, ln[O], 3 * post + 2)
                            nc.vector.tensor_scalar(veps[:, :], mv[:, 1:2], EPS, None, ALU.add).then_inc(ln[O], 1)
                            nc.vector.scalar_tensor_tensor(out=zg[:, :], in0=tsum[:, :], scalar=mv[:, 0:1], in1=gamma[O][:, :],
                                                           op0=ALU.subtract, op1=ALU.mult).then_inc(zg_ready[O], 1)
                return slot

            dve.wait_ge(flag_ok, 2)
            any_mask = dve.value_load(mflag[0:1, 0:1], min_val=0, max_val=1)
            with dve.If(any_mask == 0):
                run(dve, slots(False))
            with dve.Else():
                run(dve, slots(True))

        @block.tensor
        def _(pe):
            def slots(masked):
                def slot(L, i, has):
                    main, ahead, post, proj = units(L, i)
                    m_ok, a_ok, p_ok, j_ok = has
                    O = 1 - L
                    job_free = [(q_evac[O], NG * (ahead + 1)) if a_ok else (mt_evac[L], 2 * main + 1) if m_ok else None]

                    def take_job_bank():
                        if job_free[0] is not None:
                            need(pe, *job_free[0])

                    def scores(k):
                        chunk, groups = piece(k)
                        if k == 0 or k == HALF:
                            need(pe, m_rows[L][k // HALF], 16 * (main + 1))
                        if k >= 2:
                            need(pe, exp_done[L], PIECES * main + k - 1)
                        elif p_ok:
                            need(pe, exp_done[O], PIECES * post + PIECES - 1 + k)
                        rows = slice(KCS * chunk, KCS * chunk + KCS)
                        for j, g in enumerate(groups):
                            last = nc.tensor.matmul(sc[k % 2][0:KCS, j, 0:GL], ks[L][0:KM, g, rows], qs[L][0:KM, g, :],
                                                    start=True, stop=not masked)
                            if masked:
                                last = nc.tensor.matmul(sc[k % 2][0:KCS, j, 0:GL], mask[L][:, rows],
                                                        ident4[:, :, :].rearrange("p c l -> p (c l)"),
                                                        start=False, stop=True)
                        last.then_inc(sc_ps[L], 1)

                    def maximum(hh):
                        if hh % HH == 0:
                            need(pe, stack[O][hh // HH], 16 * NSTACK * (ahead + 1))
                        if hh >= 2:
                            need(pe, max_done[O], NH * ahead + hh - 1)
                        elif m_ok:
                            need(pe, max_done[L], NH * main + NH - 1 + hh)
                        g, c = hh // NG, hh % NG
                        nc.tensor.matmul(ms[hh % 2][0:S, 0:S2], qs[O][0:KT, g, S * c:S * c + S], ks[O][0:KT, g, :],
                                         start=True, stop=True).then_inc(ms_ps[O], 1)

                    def values(U, q, b, before):
                        half, chunk = q // KC, q % KC
                        need(pe, exp_done[U], PIECES * b + 2 * q + 2)
                        if q == 0:
                            need(pe, v_ready[U], b + 1)
                            if before is not None:
                                need(pe, pv_evac[before[0]][1], before[1] + 1)
                        if q == KC:
                            need(pe, pv_evac[U][0], b + 1)
                        for j in range(4):
                            last = nc.tensor.matmul(pv[32 * j:32 * j + 32, 0:GL], vs[U][:, chunk, 4 * half + j, :, :].rearrange("s d two -> s (d two)"),
                                                    probs[:, (2 * q + j // 2) % RING, j % 2, :],
                                                    start=(chunk == 0), stop=(chunk == KC - 1))
                        last.then_inc(pv_ps[U], 1)

                    def max_columns(U, h, b):
                        take_job_bank()
                        need(pe, m_part[U], 4 * (2 * b + h + 1))
                        nc.tensor.transpose(jobb[0:2 * PARTS * HH, 0:S], mp[:, :, :].rearrange("p a b -> p (a b)"),
                                            identb[:, :]).then_inc(mt_ps[U], 1)
                        job_free[0] = (mt_evac[U], 2 * b + h + 1)

                    def project_values(chunks):
                        if 0 in chunks:
                            take_job_bank()
                            need(pe, ctx_in[O], 16 * (ahead + 1))
                        for c in chunks:
                            for t in range(DC):
                                last = nc.tensor.matmul(job[0:KCS, P * c:P * c + P], ctxT[O][:, t, KCS * c:KCS * c + KCS],
                                                        wv[O][:, t, :], start=(t == 0), stop=(t == DC - 1))
                        if KC - 1 in chunks:
                            last.then_inc(v_ps[O], 1)
                            job_free[0] = (v_ready[O], ahead + 1)

                    def project_keys(chunks):
                        if 0 in chunks:
                            take_job_bank()
                            need(pe, ctx_in[L], 16 * (proj + 1))
                        for t in chunks:
                            last = nc.tensor.matmul(job[:, 0:S2], wk[L][:, t, :], ctxT[L][:, t, :],
                                                    start=(t == 0), stop=(t == DC - 1))
                        if DC - 1 in chunks:
                            last.then_inc(k_ps[L], 1)
                            job_free[0] = (k_evac[L], proj + 1)

                    def project_outputs(heads):
                        if 0 in heads:
                            take_job_bank()
                            need(pe, on_ready[O], post + 1)
                        for c in heads:
                            last = nc.tensor.matmul(job[0:S, 0:D], on[:, S * c:S * c + S], wo[O][:, c, :],
                                                    start=(c == 0), stop=(c == NG - 1))
                        if NG - 1 in heads:
                            last.then_inc(o_ps[O], 1)
                            job_free[0] = (o_evac[O], post + 1)

                    def transpose_rows():
                        take_job_bank()
                        need(pe, y_ready[0], post + 1)
                        for t in range(DC):
                            last = nc.tensor.transpose(job[:, S * t:S * t + S], y[0][:, P * t:P * t + P], ident[0:S, 0:S])
                        last.then_inc(t_ps, 1)
                        job_free[0] = (xT_ready, post + 1)

                    def project_queries(heads):
                        if 0 in heads:
                            take_job_bank()
                            if L == 0:
                                need(pe, xT_in, 16 * (proj + 1))
                            else:
                                need(pe, xT_ready, proj + 1)
                        for c in heads:
                            for t in range(DC):
                                last = nc.tensor.matmul(job[:, S * c:S * c + S], wq[L][:, t, c, :], xT[L][:, t, :],
                                                        start=(t == 0), stop=(t == DC - 1))
                        if NG - 1 in heads:
                            last.then_inc(q_ps[L], 1)

                    for k in range(PIECES):
                        head = iter(range(HEAD0[k], HEAD0[k + 1]) if a_ok else ())

                        def next_maximum(n=1):
                            for hh in [h for _, h in zip(range(n), head)]:
                                maximum(hh)

                        if m_ok:
                            scores(k)
                        next_maximum()
                        if k == 1 and a_ok:
                            project_values((0, 1))
                        if k == 2 and a_ok:
                            project_values((2,))
                        if k == 4 and p_ok:
                            project_outputs((0,))
                        if k == 5 and p_ok:
                            project_outputs((2,))
                        if k == 7 and j_ok:
                            project_keys((3,))
                        if k == 9 and j_ok:
                            project_queries((0,))
                        if k == 10 and j_ok:
                            project_queries((2,))
                        next_maximum()
                        if k == 0 and p_ok:
                            values(O, NPV - 1, post, None)
                        if k >= 2 and k % 2 == 0 and m_ok:
                            values(L, (k - 2) // 2, main, (O, post) if p_ok else None)
                        next_maximum()
                        if k == 0 and m_ok:
                            max_columns(L, 1, main)
                        if k == 4 and p_ok:
                            project_outputs((1,))
                        if k == 5 and p_ok:
                            project_outputs((3,))
                        if k == 6 and j_ok:
                            project_keys((0, 1, 2))
                        if k == 8 and a_ok:
                            max_columns(O, 0, ahead)
                        if k == 9 and j_ok:
                            project_queries((1,))
                        if k == 10 and j_ok:
                            project_queries((3,))
                        next_maximum(NH)
                        if k == 8 and p_ok and O == 0:
                            transpose_rows()
                return slot

            pe.wait_ge(idd, 3)
            pe.wait_ge(w_in, 16 * NW)
            pe.wait_ge(flag_col, MLOADS + 1)
            nc.tensor.transpose(job[0:1, 0:KCS], mcol[:, :], ident[0:KCS, 0:KCS]).then_inc(flag_row, 1)
            pe.wait_ge(flag_ok, 2)
            any_mask = pe.value_load(mflag[0:1, 0:1], min_val=0, max_val=1)
            with pe.If(any_mask == 0):
                run(pe, slots(False))
            with pe.Else():
                run(pe, slots(True))


def run(eng, slot):
    FIRST, STEADY, LAST = -1, 3, B - 2
    for i in range(FIRST, STEADY):
        for L in range(LAYERS):
            slot(L, i, exists(L, i))
    with eng.Fori(STEADY, LAST) as i:
        for L in range(LAYERS):
            slot(L, i, exists(L, None))
    for i in range(LAST, B + 2):
        for L in range(LAYERS):
            slot(L, i, exists(L, i))


def kernel(**inputs):
    import numpy as np
    import concourse.bacc as bacc
    from concourse.bass_utils import run_bass_kernel_spmd

    nc = bacc.Bacc("TRN2", target_bir_lowering=False, num_devices=1)
    arrays = {}

    def put(name, a):
        a = np.ascontiguousarray(a)
        arrays["in_" + name] = a
        return nc.dram_tensor("in_" + name, a.shape, mybir.dt.from_np(a.dtype), kind="ExternalInput").ap()

    x = np.asarray(inputs["x"])
    c = np.asarray(inputs["ctx_2048"])
    m = np.asarray(inputs["mask_Bx1xSxS2_ff0"])
    xT_d = put("xT", x.reshape(B, S, DC, P).transpose(0, 3, 2, 1).reshape(B, P, DC * S))
    x_d = put("x", x)
    ctxT_d = put("ctxT", c.reshape(B, S2, DC, P).transpose(0, 3, 2, 1).reshape(B, P, DC * S2))
    mask_d = put("mask", m.reshape(B, S, S2))
    mflat_d = put("mask_bits", m.reshape(MLOADS, KCS, MROW).view(np.uint32))
    W = []
    for L in range(LAYERS):
        w = {k: np.asarray(inputs[f"L{L}_xattn_{k}"])
             for k in ("Wq", "bq", "Wk", "bk", "Wv", "bv", "Wo", "bo", "gamma", "beta")}
        W.append({
            "Wq": put(f"Wq{L}", w["Wq"].reshape(DC, P, 2, 4, NG, HD).transpose(1, 0, 4, 2, 5, 3).reshape(P, DC * D)),
            "Wk": put(f"Wk{L}", w["Wk"].reshape(DC, P, 2, 4, HD).transpose(1, 0, 2, 4, 3).reshape(P, DC * P)),
            "Wv": put(f"Wv{L}", w["Wv"].reshape(DC, P, P).transpose(1, 0, 2).reshape(P, DC * P)),
            "Wo": put(f"Wo{L}", w["Wo"].reshape(NKV, NG, HD, D).transpose(0, 2, 1, 3).reshape(P, NG * D)),
            "bq": put(f"bq{L}", w["bq"].reshape(2, 4, NG, HD).transpose(0, 3, 1, 2).reshape(P, NG)),
            "bk": put(f"bk{L}", w["bk"].reshape(2, 4, HD).transpose(0, 2, 1).reshape(P, 1)),
            "bv": put(f"bv{L}", w["bv"].reshape(1, P)),
            "bo": put(f"bo{L}", w["bo"].reshape(1, D)),
            "gamma": put(f"gamma{L}", w["gamma"].reshape(1, D)),
            "beta": put(f"beta{L}", w["beta"].reshape(1, D)),
        })
    out = nc.dram_tensor("out", (B, S, D), F32, kind="ExternalOutput").ap()
    cross_attention_two_layers(nc, xT_d, x_d, ctxT_d, mask_d, mflat_d, W, out)
    r = run_bass_kernel_spmd(nc, [arrays], core_ids=[0])
    return r.results[0]["out"]
```

```python
import concourse.bass as bass
from concourse import mybir
from contextlib import ExitStack

F32 = mybir.dt.float32
BF16 = mybir.dt.bfloat16
U32 = mybir.dt.uint32
I32 = mybir.dt.int32
ALU = mybir.AluOpType
ACT = mybir.ActivationFunctionType
AX_X = mybir.AxisListType.X

B, S, S2, D = 32, 112, 375, 512
NH, NKV, HD = 32, 8, 16
NG = NH // NKV
LAYERS = 2
P = 128
DC = D // P
KC = 3
KCS = S2 // KC
GL = NG * S
SCALE = float(HD) ** -0.5
EPS = 1e-6
LOWEST = -3.0e38

TERMS = [(0, 0), (0, 1), (1, 0), (1, 1), (0, 2), (2, 0)]
NT = len(TERMS)
KT = NT * HD
PARTS = 3
KM = KT + PARTS

MLOADS = 4
MROW = B * S * S2 // (MLOADS * KCS)
assert MROW * MLOADS * KCS == B * S * S2

PIECES = 12
HALF = PIECES // 2
NPV = PIECES // 2
RING = 6
HEADS_AT = [0, 0, 0, 2, 3, 4, 4, 3, 3, 5, 5, 3]
VALUES_AT = [2, 4, 7, 8, 10]
HEAD0 = [sum(HEADS_AT[:k]) for k in range(PIECES + 1)]
HH = NH // 2
NSTACK = 2 * NT
assert KCS * KC == S2 and HEAD0[-1] == NH and KM <= P and HEAD0[8] == HH


def units(L, i):
    main = i if L == 0 else i - 1
    ahead = i - 1 if L == 0 else i + 1
    post = ahead - 1
    proj = main + 1
    return main, ahead, post, proj


def exists(L, i):
    if i is None:
        return True, True, True, True
    return tuple(0 <= b < B for b in units(L, i))


def need(eng, sem, value):
    if isinstance(value, int) and value <= 0:
        return
    eng.wait_ge(sem, value)


def piece(k):
    half, chunk, pair = k // HALF, (k % HALF) // 2, k % 2
    return chunk, [4 * half + 2 * pair + j for j in range(2)]


def cross_attention_two_layers(nc, xT_d, x_d, ctxT_d, mask_d, mflat_d, W, out):
    with ExitStack() as ctx:
        def sb(name, shape, dt=F32):
            return ctx.enter_context(nc.sbuf_tensor(name, shape, dt))

        def ps(name, shape, dt=F32):
            return ctx.enter_context(nc.psum_tensor(name, shape, dt))

        def sem(name):
            return ctx.enter_context(nc.semaphore(name))

        def per_layer(make, name, *a):
            return [make(f"{name}{L}", *a) for L in range(LAYERS)]

        wq = per_layer(sb, "wq", [P, DC, NG, P])
        wk = per_layer(sb, "wk", [P, DC, P])
        wv = per_layer(sb, "wv", [P, DC, P])
        wo = per_layer(sb, "wo", [P, NG, D])
        bq = per_layer(sb, "bq", [P, NG])
        bqs = per_layer(sb, "bqs", [P, NG])
        bk = per_layer(sb, "bk", [P, 1])
        bv = per_layer(sb, "bv", [KCS, P])
        bo = per_layer(sb, "bo", [S, D])
        gamma = per_layer(sb, "gamma", [S, D])
        beta = per_layer(sb, "beta", [S, D])
        ident = sb("ident", [P, P])
        ident4 = sb("ident4", [S, NG, S])
        negident = sb("negident", [S, S], BF16)
        neghalf = sb("neghalf", [S, 1])
        zero = sb("zero", [S, 1])
        pause = sb("pause", [S, 1])
        mcols = sb("mcols", [KCS, MLOADS])
        mcol = sb("mcol", [KCS, 1])
        mrow = sb("mrow", [1, 2])
        mflag = sb("mflag", [1, 1], I32)
        ctxT = per_layer(sb, "ctxT", [P, DC, S2])
        xT = per_layer(sb, "xT", [P, DC, S])
        xin = sb("xin", [S, D])
        mask = per_layer(sb, "mask", [S, S2])
        qf = sb("qf", [P, GL])
        qr = sb("qr", [P, GL])
        qp = sb("qp", [P, PARTS, GL], BF16)
        kf = sb("kf", [P, S2])
        kr = sb("kr", [P, S2])
        kp = per_layer(sb, "kp", [P, PARTS, S2], BF16)
        qs = per_layer(sb, "qs", [P, NKV, GL], BF16)
        ks = per_layer(sb, "ks", [P, NKV, S2], BF16)
        vs = per_layer(sb, "vs", [KCS, KC, NKV, HD, 2])
        scratch = sb("scratch", [S, S2])
        mx = per_layer(sb, "mx", [S, NH])
        mr = sb("mr", [S, HH])
        mp = sb("mp", [S, PARTS, HH], BF16)
        mT = sb("mT", [PARTS * HH, S], BF16)
        probs = sb("probs", [KCS, RING, 2, GL])
        mbits = probs[:, :, :, :].rearrange("p a b c -> p (a b c)").bitcast(U32)
        oraw = [sb(f"oraw{h}", [P, GL]) for h in range(2)]
        oc = sb("oc", [P, GL])
        osum = sb("osum", [P, GL])
        orec = sb("orec", [P, GL])
        on = sb("on", [P, GL])
        res = per_layer(sb, "res", [S, D])
        tsum = sb("tsum", [S, D])
        stats = sb("stats", [S, 6])
        mv = sb("mv", [S, 2])
        veps = sb("veps", [S, 1])
        rstd = sb("rstd", [S, 1])
        zg = sb("zg", [S, D])
        y = per_layer(sb, "y", [S, D])

        sc = [ps(f"sc{h}", [P, 2, 512]) for h in range(2)]
        ms = [ps(f"ms{h}", [P, 512]) for h in range(2)]
        pv = ps("pv", [P, 512])
        job = ps("job", [P, 512])

        w_in = sem("w_in")
        mf_in = [sem(f"mf_in{n}") for n in range(2)]
        consts = sem("consts")
        ids = sem("ids")
        idd = sem("idd")
        flag_col = sem("flag_col")
        flag_row = sem("flag_row")
        flag_ok = sem("flag_ok")
        ctx_in = per_layer(sem, "ctx_in")
        mask_in = per_layer(sem, "mask_in")
        xT_in = sem("xT_in")
        x_in = sem("x_in")
        k_ps = per_layer(sem, "k_ps")
        v_ps = per_layer(sem, "v_ps")
        q_ps = per_layer(sem, "q_ps")
        o_ps = per_layer(sem, "o_ps")
        t_ps = sem("t_ps")
        mt_ps = per_layer(sem, "mt_ps")
        k_evac = per_layer(sem, "k_evac")
        q_evac = per_layer(sem, "q_evac")
        k_p1 = per_layer(sem, "k_p1")
        k_r = per_layer(sem, "k_r")
        k_p2 = per_layer(sem, "k_p2")
        k_p3 = per_layer(sem, "k_p3")
        q_p1 = per_layer(sem, "q_p1")
        q_r = per_layer(sem, "q_r")
        q_p2 = per_layer(sem, "q_p2")
        q_p3 = per_layer(sem, "q_p3")
        v_ready = per_layer(sem, "v_ready")
        xT_ready = sem("xT_ready")
        stack = [[sem(f"stack{L}{h}") for h in range(2)] for L in range(LAYERS)]
        m_rows = [[sem(f"m_rows{L}{h}") for h in range(2)] for L in range(LAYERS)]
        ms_ps = per_layer(sem, "ms_ps")
        m_masked = per_layer(sem, "m_masked")
        max_done = per_layer(sem, "max_done")
        m_part = per_layer(sem, "m_part")
        mt_evac = per_layer(sem, "mt_evac")
        sc_ps = per_layer(sem, "sc_ps")
        exp_done = per_layer(sem, "exp_done")
        pv_ps = per_layer(sem, "pv_ps")
        pv_evac = [[sem(f"pv_evac{L}{h}") for h in range(2)] for L in range(LAYERS)]
        o_in = per_layer(sem, "o_in")
        sum_in = per_layer(sem, "sum_in")
        o_rec = per_layer(sem, "o_rec")
        on_ready = per_layer(sem, "on_ready")
        res_ready = per_layer(sem, "res_ready")
        o_evac = per_layer(sem, "o_evac")
        ln = per_layer(sem, "ln")
        rs_ready = per_layer(sem, "rs_ready")
        zg_ready = per_layer(sem, "zg_ready")
        y_ready = per_layer(sem, "y_ready")
        out_done = sem("out_done")

        NW = 10 * LAYERS
        block = ctx.enter_context(nc.Block())

        @block.sync
        def _(sp):
            def load_ctx(L, b):
                sp.dma_start(ctxT[L][:, :, :].rearrange("p a b -> p (a b)"), ctxT_d[b]).then_inc(ctx_in[L], 16)

            def load_mask(L, b):
                sp.dma_start(mask[L][:, :], mask_d[b]).then_inc(mask_in[L], 16)

            def load_xT(b):
                sp.dma_start(xT[0][:, :, :].rearrange("p a b -> p (a b)"), xT_d[b]).then_inc(xT_in, 16)

            def load_x(b):
                sp.dma_start(xin[:, :], x_d[b]).then_inc(x_in, 16)

            def stack_terms(L, h, dst, src, which, of=range(PARTS)):
                for t, parts in enumerate(TERMS):
                    if parts[which] not in of:
                        continue
                    sp.dma_start(dst[HD * t:HD * t + HD, 4 * h:4 * h + 4, :].rearrange("d g n -> d (g n)"),
                                 src[64 * h:64 * h + 64, parts[which], :]).then_inc(stack[L][h], 16)

            def max_rows(L, h, count):
                sp.wait_ge(mt_evac[L], count)
                sp.dma_start(qs[L][KT:KM, 4 * h:4 * h + 4, :].rearrange("p g n -> p (g n)"), mT[:, :])\
                  .then_inc(m_rows[L][h], 16)

            def outputs(L, h, count):
                sp.wait_ge(pv_evac[L][h], count)
                sp.dma_start(osum[64 * h:64 * h + 64, :], oraw[h][1::2, :]).then_inc(sum_in[L], 16)
                sp.dma_start(oc[64 * h:64 * h + 64, :], oraw[h][0::2, :]).then_inc(o_in[L], 16)

            def slot(L, i, has):
                main, ahead, post, proj = units(L, i)
                m_ok, a_ok, p_ok, j_ok = has
                O = 1 - L

                def count(value):
                    return value if isinstance(value, int) else sp.snap(value)

                mains, projs, aheads = count(main), count(proj), count(ahead)
                projs1, aheads1 = count(proj + 1), count(ahead + 1)
                main_half2 = count(2 * main + 2)
                ahead_half1 = count(2 * ahead + 1)
                post_scores = count(PIECES * ahead)
                normalized = count(2 * ahead)
                queries_proj, queries_ahead = count(2 * proj + 2), count(2 * ahead + 2)
                if a_ok:
                    sp.wait_ge(q_p3[O], queries_ahead)
                    stack_terms(O, 0, qs[O], qp, 0, of=(2,))
                if p_ok:
                    outputs(O, 1, aheads)
                if a_ok:
                    need(sp, sc_ps[O], post_scores)
                    load_mask(O, aheads)
                    stack_terms(O, 1, ks[O], kp[O], 1)
                if m_ok:
                    max_rows(L, 1, main_half2)
                if a_ok:
                    stack_terms(O, 1, qs[O], qp, 0)
                if L == 0 and j_ok:
                    need(sp, q_ps[0], projs)
                    load_xT(projs)
                if L == 0 and m_ok:
                    need(sp, res_ready[0], mains)
                    load_x(mains)
                if a_ok and not (isinstance(ahead, int) and ahead + 1 >= B):
                    sp.wait_ge(v_ps[O], aheads1)
                    load_ctx(O, aheads1)
                if m_ok:
                    if p_ok:
                        sp.wait_ge(on_ready[O], normalized)
                    outputs(L, 0, projs)
                if a_ok:
                    max_rows(O, 0, ahead_half1)
                if p_ok and O == 1:
                    sp.wait_ge(y_ready[1], aheads)
                    sp.dma_start(out[post], y[1][:, :]).then_inc(out_done, 16)
                if j_ok:
                    sp.wait_ge(k_p3[L], projs1)
                    stack_terms(L, 0, ks[L], kp[L], 1)
                    sp.wait_ge(q_p1[L], queries_proj)
                    stack_terms(L, 0, qs[L], qp, 0, of=(0,))
                    sp.wait_ge(q_p2[L], queries_proj)
                    stack_terms(L, 0, qs[L], qp, 0, of=(1,))

            def load_rows(L):
                for dst, key in ((bv, "bv"), (bo, "bo"), (gamma, "gamma"), (beta, "beta")):
                    n = dst[L].shape[0]
                    sp.dma_start(dst[L][:, :], W[L][key].to_broadcast([n, dst[L].shape[1]])).then_inc(w_in, 16)

            for L in range(LAYERS):
                sp.dma_start(wk[L][:, :, :].rearrange("p a b -> p (a b)"), W[L]["Wk"]).then_inc(w_in, 16)
                load_ctx(L, 0)
                sp.dma_start(wq[L][:, :, :, :].rearrange("p a b c -> p (a b c)"), W[L]["Wq"]).then_inc(w_in, 16)
                sp.dma_start(wv[L][:, :, :].rearrange("p a b -> p (a b)"), W[L]["Wv"]).then_inc(w_in, 16)
                sp.dma_start(wo[L][:, :, :].rearrange("p a b -> p (a b)"), W[L]["Wo"]).then_inc(w_in, 16)
                sp.dma_start(bq[L][:, :], W[L]["bq"]).then_inc(w_in, 16)
                sp.dma_start(bk[L][:, :], W[L]["bk"]).then_inc(w_in, 16)
                load_rows(L)
            for n in range(MLOADS):
                need(sp, flag_col, n - 1)
                sp.dma_start(mbits[:, MROW * (n % 2):MROW * (n % 2 + 1)], mflat_d[n]).then_inc(mf_in[n % 2], 16)
            sp.wait_ge(consts, 1)
            run(sp, slot)
            sp.wait_ge(out_done, 16 * B)

        @block.gpsimd
        def _(pool):
            nc.gpsimd.memset(ident[:, :], 0.0).then_inc(ids, 1)
            nc.gpsimd.memset(ident4[:, :, :], 0.0).then_inc(ids, 1)
            nc.gpsimd.memset(negident[:, :], 0.0).then_inc(ids, 1)
            nc.gpsimd.memset(zero[:, :], 0.0).then_inc(ids, 1)
            nc.gpsimd.memset(neghalf[:, :], -0.5).then_inc(ids, 1)
            pool.wait_ge(ids, 5)
            nc.gpsimd.affine_select(out=ident[:, :], in_=ident[:, :], compare_op=ALU.not_equal, fill=1.0,
                                    base=0, pattern=[[-1, P]], channel_multiplier=1).then_inc(idd, 1)
            nc.gpsimd.affine_select(out=ident4[:, :, :], in_=ident4[:, :, :], compare_op=ALU.not_equal, fill=1.0,
                                    base=0, pattern=[[0, NG], [-1, S]], channel_multiplier=1).then_inc(idd, 1)

            nc.gpsimd.affine_select(out=negident[:, :], in_=negident[:, :], compare_op=ALU.not_equal, fill=-1.0,
                                    base=0, pattern=[[-1, S]], channel_multiplier=1).then_inc(idd, 1)

            def slot(L, i, has):
                main, ahead, post, proj = units(L, i)
                m_ok, a_ok, p_ok, j_ok = has
                O = 1 - L

                def max_parts(U, h, b):
                    cols = mx[U][:, HH * h:HH * h + HH]
                    done = 4 * (2 * b + h)
                    pool.wait_ge(max_done[U], NH * b + HH * (h + 1))
                    if h == 1:
                        pool.wait_ge(mt_ps[U], 2 * b + 1)
                    elif m_ok:
                        pool.wait_ge(mt_ps[L], 2 * main + 2)
                    nc.gpsimd.tensor_tensor(mp[:, 0, :], cols, zero[:, :].to_broadcast([S, HH]), ALU.add).then_inc(m_part[U], 1)
                    pool.wait_ge(m_part[U], done + 1)
                    nc.gpsimd.tensor_tensor(mr[:, :], cols, mp[:, 0, :], ALU.subtract).then_inc(m_part[U], 1)
                    pool.wait_ge(m_part[U], done + 2)
                    nc.gpsimd.tensor_tensor(mp[:, 1, :], mr[:, :], zero[:, :].to_broadcast([S, HH]), ALU.add).then_inc(m_part[U], 1)
                    pool.wait_ge(m_part[U], done + 3)
                    nc.gpsimd.tensor_tensor(mp[:, 2, :], mr[:, :], mp[:, 1, :], ALU.subtract)\
                      .then_inc(m_part[U], 1)

                if m_ok:
                    max_parts(L, 1, main)
                if p_ok and O == 0:
                    pool.wait_ge(x_in, 16 * (post + 1))
                    need(pool, o_evac[0], post)
                    nc.gpsimd.tensor_tensor(res[0][:, :], xin[:, :], bo[0][:, :], ALU.add).then_inc(res_ready[0], 1)
                if p_ok:
                    for h in range(2):
                        cols = slice(GL // 2 * h, GL // 2 * (h + 1))
                        if h == 0:
                            pool.wait_ge(o_in[O], 32 * (post + 1))
                        pool.wait_ge(o_rec[O], 4 * post + 2 * h + 2)
                        nc.gpsimd.tensor_tensor(on[:, cols], oc[:, cols], orec[:, cols], ALU.mult)\
                          .then_inc(on_ready[O], 1)
                if j_ok:
                    pool.wait_ge(k_p1[L], proj + 1)
                    nc.gpsimd.tensor_tensor(kr[:, :], kf[:, :], kp[L][:, 0, :], ALU.subtract).then_inc(k_r[L], 1)
                    pool.wait_ge(k_p2[L], proj + 1)
                    nc.gpsimd.tensor_tensor(kp[L][:, 2, :], kr[:, :], kp[L][:, 1, :], ALU.subtract).then_inc(k_p3[L], 1)
                if p_ok:
                    pool.wait_ge(ln[O], 3 * (post + 1))
                    nc.gpsimd.tensor_tensor(rstd[:, :], veps[:, :], neghalf[:, :], ALU.pow).then_inc(rs_ready[O], 1)
                if a_ok:
                    max_parts(O, 0, ahead)
                if a_ok and O == 1:
                    pool.wait_ge(y_ready[0], ahead + 1)
                    need(pool, o_evac[1], ahead)
                    nc.gpsimd.tensor_tensor(res[1][:, :], y[0][:, :], bo[1][:, :], ALU.add).then_inc(res_ready[1], 1)
                if j_ok:
                    for h in range(2):
                        cols = slice(GL // 2 * h, GL // 2 * (h + 1))
                        pool.wait_ge(q_p1[L], 2 * proj + h + 1)
                        nc.gpsimd.tensor_tensor(qr[:, cols], qf[:, cols], qp[:, 0, cols], ALU.subtract)\
                          .then_inc(q_r[L], 1)
                    for h in range(2):
                        cols = slice(GL // 2 * h, GL // 2 * (h + 1))
                        pool.wait_ge(q_p2[L], 2 * proj + h + 1)
                        nc.gpsimd.tensor_tensor(qp[:, 2, cols], qr[:, cols], qp[:, 1, cols], ALU.subtract)\
                          .then_inc(q_p3[L], 1)

            pool.wait_ge(w_in, 16 * NW)
            run(pool, slot)

        @block.scalar
        def _(act):
            def slot(L, i, has):
                main, ahead, post, proj = units(L, i)
                m_ok, a_ok, p_ok, j_ok = has
                O = 1 - L

                def exp(k):
                    if not m_ok:
                        return
                    act.wait_ge(sc_ps[L], PIECES * main + k + 1)
                    if k >= RING:
                        act.wait_ge(pv_ps[L], NPV * main + (k - RING) // 2 + 1)
                    elif p_ok:
                        act.wait_ge(pv_ps[O], NPV * post + (PIECES - RING + k) // 2 + 1)
                    nc.scalar.activation(probs[:, k % RING, :, :], sc[k % 2][0:KCS, :, 0:GL], ACT.Exp)\
                      .then_inc(exp_done[L], 1)

                def pv_out(U, h, b, before):
                    act.wait_ge(pv_ps[U], NPV * b + 3 * (h + 1))
                    if before is not None:
                        act.wait_ge(sum_in[before[0]], 32 * (before[1] + 1))
                        act.wait_ge(o_in[before[0]], 32 * (before[1] + 1))
                    nc.scalar.copy(oraw[h][:, :], pv[:, 0:GL]).then_inc(pv_evac[U][h], 1)

                def m_out(U, h, b, rows):
                    act.wait_ge(mt_ps[U], 2 * b + h + 1)
                    if rows is not None:
                        need(act, m_rows[rows[0]][1 - h], 16 * rows[1])
                    nc.scalar.copy(mT[:, :], job[0:PARTS * HH, 0:S]).then_inc(mt_evac[U], 1)

                for k in range(PIECES):
                    if k == 9 and p_ok and O == 0:
                        act.wait_ge(t_ps, post + 1)
                        need(act, q_ps[1], post)
                        nc.scalar.copy(xT[1][:, :, :].rearrange("p a b -> p (a b)"), job[:, 0:GL])\
                          .then_inc(xT_ready, 1)
                    if k == 0 and p_ok:
                        first, last = isinstance(main, int) and main < 1, isinstance(main, int) and main > B
                        pv_out(O, 1, post, (O, post - 1) if last else None if first else (L, main - 1))
                    if k == 4 and j_ok:
                        act.wait_ge(k_ps[L], proj + 1)
                        if a_ok:
                            act.wait_ge(k_r[O], ahead + 1)
                        if m_ok:
                            act.wait_ge(stack[L][0], 16 * NSTACK * (main + 1))
                            act.wait_ge(stack[L][1], 16 * NSTACK * (main + 1))
                        nc.scalar.activation(kf[:, :], job[:, 0:S2], ACT.Identity, bias=bk[L][:, 0:1])\
                          .then_inc(k_evac[L], 1)
                        act.wait_ge(k_evac[L], proj + 1)
                        nc.scalar.copy(kp[L][:, 0, :], kf[:, :]).then_inc(k_p1[L], 1)
                    exp(k)
                    if k == 2 and m_ok:
                        m_out(L, 1, main, (L, main + 1))
                    if k == 5 and j_ok:
                        act.wait_ge(k_r[L], proj + 1)
                        nc.scalar.copy(kp[L][:, 1, :], kr[:, :]).then_inc(k_p2[L], 1)
                    if k == 7 and m_ok:
                        pv_out(L, 0, main, (O, post) if p_ok else None)
                    if k == 8 and a_ok:
                        m_out(O, 0, ahead, (L, main + 1) if m_ok else None)
                    if k == 10 and j_ok:
                        act.wait_ge(q_ps[L], proj + 1)
                        if a_ok:
                            act.wait_ge(q_r[O], 2 * (ahead + 1))
                            act.wait_ge(stack[O][0], 16 * NSTACK * (ahead + 1))
                            act.wait_ge(stack[O][1], 16 * NSTACK * (ahead + 1))
                        for c in range(NG):
                            nc.scalar.activation(qf[:, S * c:S * c + S], job[:, S * c:S * c + S], ACT.Identity,
                                                 bias=bqs[L][:, c:c + 1], scale=SCALE).then_inc(q_evac[L], 1)
                        for h in range(2):
                            cols = slice(GL // 2 * h, GL // 2 * (h + 1))
                            act.wait_ge(q_evac[L], NG * proj + 2 * h + 2)
                            nc.scalar.copy(qp[:, 0, cols], qf[:, cols]).then_inc(q_p1[L], 1)
                if j_ok:
                    for h in range(2):
                        cols = slice(GL // 2 * h, GL // 2 * (h + 1))
                        act.wait_ge(q_r[L], 2 * proj + h + 1)
                        nc.scalar.copy(qp[:, 1, cols], qr[:, cols]).then_inc(q_p2[L], 1)

            act.wait_ge(w_in, 16 * NW)
            act.wait_ge(consts, 1 + LAYERS)
            run(act, slot)

        @block.vector
        def _(dve):
            for L in range(LAYERS):
                nc.vector.memset(qs[L][:, :, :].bitcast(U32), 0)
                nc.vector.memset(ks[L][:, :, :], 1.0)
                last = nc.vector.memset(vs[L][:, :, :, :, 1], 1.0)
            last.then_inc(consts, 1)
            dve.wait_ge(w_in, 16 * NW)
            for L in range(LAYERS):
                nc.vector.tensor_scalar(bqs[L][:, :], bq[L][:, :], SCALE, None, ALU.mult).then_inc(consts, 1)
            for n in range(MLOADS):
                dve.wait_ge(mf_in[n % 2], 16 * (n // 2 + 1))
                nc.vector.tensor_reduce(mcols[:, n:n + 1], mbits[:, MROW * (n % 2):MROW * (n % 2 + 1)], AX_X, ALU.max).then_inc(flag_col, 1)
            dve.wait_ge(flag_col, MLOADS)
            nc.vector.tensor_reduce(mcol[:, :], mcols[:, :], AX_X, ALU.max).then_inc(flag_col, 1)
            dve.wait_ge(flag_row, 1)
            nc.vector.tensor_reduce(mrow[:, 0:1], job[0:1, 0:KCS], AX_X, ALU.max).then_inc(flag_ok, 1)
            dve.wait_ge(flag_ok, 1)
            nc.vector.tensor_scalar(mflag[:, :], mrow[:, 0:1], 0.0, None, ALU.is_gt).then_inc(flag_ok, 1)

            def slots(masked):
                def slot(L, i, has):
                    main, ahead, post, proj = units(L, i)
                    m_ok, a_ok, p_ok, j_ok = has
                    O = 1 - L

                    def maximum(hh):
                        dve.wait_ge(ms_ps[O], NH * ahead + hh + 1)
                        if masked:
                            nc.vector.tensor_tensor(scratch[:, :], ms[hh % 2][0:S, 0:S2], mask[O][:, :], ALU.add)\
                              .then_inc(m_masked[O], 1)
                            dve.wait_ge(m_masked[O], NH * ahead + hh + 1)
                            nc.vector.tensor_reduce(mx[O][:, hh:hh + 1], scratch[:, :], AX_X, ALU.max)\
                              .then_inc(max_done[O], 1)
                            dve.wait_ge(max_done[O], NH * ahead + hh + 1)
                        else:
                            nc.vector.tensor_reduce(mx[O][:, hh:hh + 1], ms[hh % 2][0:S, 0:S2], AX_X, ALU.max)\
                              .then_inc(max_done[O], 1)

                    def reciprocal(n):
                        if n == 0:
                            dve.wait_ge(sum_in[O], 32 * (post + 1))
                        nc.vector.reciprocal(orec[:, S * n:S * n + S], osum[:, S * n:S * n + S])\
                          .then_inc(o_rec[O], 1)

                    def statistics():
                        dve.wait_ge(o_evac[O], post + 1)
                        nc.vector.bn_stats(stats[:, :], tsum[:, :]).then_inc(ln[O], 1)

                    def deviation():
                        dve.wait_ge(ln[O], 3 * post + 1)
                        nc.vector.memset(pause[:, :], 0.0)
                        nc.vector.bn_aggr(mv[:, :], stats[:, :]).then_inc(ln[O], 1)
                        dve.wait_ge(ln[O], 3 * post + 2)
                        nc.vector.tensor_scalar(veps[:, :], mv[:, 1:2], EPS, None, ALU.add).then_inc(ln[O], 1)

                    def result_rows():
                        dve.wait_ge(rs_ready[O], post + 1)
                        dve.wait_ge(zg_ready[O], post + 1)
                        if O == 1:
                            need(dve, out_done, 16 * post)
                        else:
                            need(dve, t_ps, post)
                            need(dve, res_ready[1], post)
                        nc.vector.scalar_tensor_tensor(out=y[O][:, :], in0=zg[:, :], scalar=rstd[:, 0:1], in1=beta[O][:, :],
                                                       op0=ALU.mult, op1=ALU.add).then_inc(y_ready[O], 1)

                    for k in range(PIECES):
                        if k == 2 and a_ok:
                            dve.wait_ge(v_ps[O], ahead + 1)
                            if p_ok:
                                dve.wait_ge(pv_ps[O], NPV * (post + 1))
                            nc.vector.tensor_tensor(
                                vs[O][:, :, :, :, 0], job[0:KCS, 0:KC * P].rearrange("p (c g d) -> p c g d", c=KC, d=HD),
                                bv[O][:, :].rearrange("p (g d) -> p g d", d=HD).unsqueeze(1)
                                .to_broadcast([KCS, KC, NKV, HD]), ALU.add).then_inc(v_ready[O], 1)
                        if k == 7 and p_ok:
                            dve.wait_ge(o_ps[O], post + 1)
                            dve.wait_ge(res_ready[O], post + 1)
                            nc.vector.tensor_tensor(tsum[:, :], job[0:S, 0:D], res[O][:, :], ALU.add)\
                              .then_inc(o_evac[O], 1)
                        if a_ok:
                            if k == (3 if masked else 7):
                                dve.wait_ge(mask_in[O], 16 * (ahead + 1))
                        for hh in range(HEAD0[k], HEAD0[k + 1]):
                            if a_ok:
                                maximum(hh)
                            step = hh - HEAD0[k]
                            if k in (3, 4) and p_ok and step < 2:
                                reciprocal(2 * (k - 3) + step)
                            if k == 7 and p_ok and step == 0:
                                statistics()
                            if k == 7 and p_ok and step == 1:
                                deviation()
                            if k == 8 and p_ok and step == 0:
                                result_rows()
                        if k == 7 and p_ok:
                            nc.vector.scalar_tensor_tensor(out=zg[:, :], in0=tsum[:, :], scalar=mv[:, 0:1], in1=gamma[O][:, :],
                                                           op0=ALU.subtract, op1=ALU.mult).then_inc(zg_ready[O], 1)
                return slot

            dve.wait_ge(flag_ok, 2)
            any_mask = dve.value_load(mflag[0:1, 0:1], min_val=0, max_val=1)
            with dve.If(any_mask == 0):
                run(dve, slots(False))
            with dve.Else():
                run(dve, slots(True))

        @block.tensor
        def _(pe):
            def slots(masked):
                def slot(L, i, has):
                    main, ahead, post, proj = units(L, i)
                    m_ok, a_ok, p_ok, j_ok = has
                    O = 1 - L
                    job_free = [(q_evac[O], NG * (ahead + 1)) if a_ok else (mt_evac[L], 2 * main + 1) if m_ok else None]

                    def take_job_bank():
                        if job_free[0] is not None:
                            pe.wait_ge(*job_free[0])

                    def scores(k):
                        chunk, groups = piece(k)
                        if k == 0 or k == HALF:
                            pe.wait_ge(m_rows[L][k // HALF], 16 * (main + 1))
                        if k >= 2:
                            pe.wait_ge(exp_done[L], PIECES * main + k - 1)
                        elif p_ok:
                            pe.wait_ge(exp_done[O], PIECES * post + PIECES - 1 + k)
                        rows = slice(KCS * chunk, KCS * chunk + KCS)
                        for j, g in enumerate(groups):
                            last = nc.tensor.matmul(sc[k % 2][0:KCS, j, 0:GL], ks[L][0:KM, g, rows], qs[L][0:KM, g, :],
                                                    start=True, stop=not masked)
                            if masked:
                                last = nc.tensor.matmul(sc[k % 2][0:KCS, j, 0:GL], mask[L][:, rows],
                                                        ident4[:, :, :].rearrange("p c l -> p (c l)"),
                                                        start=False, stop=True)
                        last.then_inc(sc_ps[L], 1)

                    def maximum(hh):
                        if hh % HH == 0:
                            pe.wait_ge(stack[O][hh // HH], 16 * NSTACK * (ahead + 1))
                        if hh >= 2:
                            pe.wait_ge(max_done[O], NH * ahead + hh - 1)
                        elif m_ok:
                            pe.wait_ge(max_done[L], NH * main + NH - 1 + hh)
                        g, c = hh // NG, hh % NG
                        nc.tensor.matmul(ms[hh % 2][0:S, 0:S2], qs[O][0:KT, g, S * c:S * c + S], ks[O][0:KT, g, :],
                                         start=True, stop=True).then_inc(ms_ps[O], 1)

                    def values(U, q, b, before):
                        half, chunk = q // KC, q % KC
                        pe.wait_ge(exp_done[U], PIECES * b + 2 * q + 2)
                        if q == 0:
                            pe.wait_ge(v_ready[U], b + 1)
                            if before is not None:
                                pe.wait_ge(pv_evac[before[0]][1], before[1] + 1)
                        if q == KC:
                            pe.wait_ge(pv_evac[U][0], b + 1)
                        for j in range(4):
                            last = nc.tensor.matmul(pv[32 * j:32 * j + 32, 0:GL], vs[U][:, chunk, 4 * half + j, :, :].rearrange("s d two -> s (d two)"),
                                                    probs[:, (2 * q + j // 2) % RING, j % 2, :],
                                                    start=(chunk == 0), stop=(chunk == KC - 1))
                        last.then_inc(pv_ps[U], 1)

                    def max_columns(U, h, b):
                        take_job_bank()
                        pe.wait_ge(m_part[U], 4 * (2 * b + h + 1))
                        nc.tensor.matmul(job[0:PARTS * HH, 0:S], mp[:, :, :].rearrange("p a b -> p (a b)"), negident[:, :],
                                         start=True, stop=True).then_inc(mt_ps[U], 1)
                        job_free[0] = (mt_evac[U], 2 * b + h + 1)

                    def project_values(chunks):
                        if 0 in chunks:
                            take_job_bank()
                            pe.wait_ge(ctx_in[O], 16 * (ahead + 1))
                        for c in chunks:
                            for t in range(DC):
                                last = nc.tensor.matmul(job[0:KCS, P * c:P * c + P], ctxT[O][:, t, KCS * c:KCS * c + KCS],
                                                        wv[O][:, t, :], start=(t == 0), stop=(t == DC - 1))
                        if KC - 1 in chunks:
                            last.then_inc(v_ps[O], 1)
                            job_free[0] = (v_ready[O], ahead + 1)

                    def project_keys(chunks):
                        if 0 in chunks:
                            take_job_bank()
                            pe.wait_ge(ctx_in[L], 16 * (proj + 1))
                        for t in chunks:
                            last = nc.tensor.matmul(job[:, 0:S2], wk[L][:, t, :], ctxT[L][:, t, :],
                                                    start=(t == 0), stop=(t == DC - 1))
                        if DC - 1 in chunks:
                            last.then_inc(k_ps[L], 1)
                            job_free[0] = (k_evac[L], proj + 1)

                    def project_outputs(heads):
                        if 0 in heads:
                            take_job_bank()
                            pe.wait_ge(on_ready[O], 2 * post + 1)
                        if 2 in heads:
                            pe.wait_ge(on_ready[O], 2 * post + 2)
                        for c in heads:
                            last = nc.tensor.matmul(job[0:S, 0:D], on[:, S * c:S * c + S], wo[O][:, c, :],
                                                    start=(c == 0), stop=(c == NG - 1))
                        if NG - 1 in heads:
                            last.then_inc(o_ps[O], 1)
                            job_free[0] = (o_evac[O], post + 1)

                    def transpose_rows():
                        take_job_bank()
                        pe.wait_ge(y_ready[0], post + 1)
                        for t in range(DC):
                            last = nc.tensor.transpose(job[:, S * t:S * t + S], y[0][:, P * t:P * t + P], ident[0:S, 0:S])
                        last.then_inc(t_ps, 1)
                        job_free[0] = (xT_ready, post + 1)

                    def project_queries(heads):
                        if 0 in heads:
                            take_job_bank()
                            if L == 0:
                                pe.wait_ge(xT_in, 16 * (proj + 1))
                            else:
                                pe.wait_ge(xT_ready, proj + 1)
                        for c in heads:
                            for t in range(DC):
                                last = nc.tensor.matmul(job[:, S * c:S * c + S], wq[L][:, t, c, :], xT[L][:, t, :],
                                                        start=(t == 0), stop=(t == DC - 1))
                        if NG - 1 in heads:
                            last.then_inc(q_ps[L], 1)

                    for k in range(PIECES):
                        head = iter(range(HEAD0[k], HEAD0[k + 1]) if a_ok else ())

                        def next_maximum(n=1):
                            for hh in [h for _, h in zip(range(n), head)]:
                                maximum(hh)

                        if m_ok:
                            scores(k)
                        next_maximum()
                        if k == 1 and a_ok:
                            project_values((1, 2))
                        if k == 3 and j_ok:
                            project_keys((0, 1))
                        if k == 5 and p_ok:
                            project_outputs((0,))
                        if k == 6 and p_ok:
                            project_outputs((2,))
                        if k == 9 and j_ok:
                            project_queries((0,))
                        if k == 10 and j_ok:
                            project_queries((2,))
                        next_maximum()
                        if k == 0 and p_ok:
                            values(O, NPV - 1, post, None)
                        if k in VALUES_AT and m_ok:
                            values(L, VALUES_AT.index(k), main, (O, post) if p_ok else None)
                        next_maximum()
                        if k == 0 and a_ok:
                            project_values((0,))
                        if k == 2 and m_ok:
                            max_columns(L, 1, main)
                        if k == 3 and j_ok:
                            project_keys((2, 3))
                        if k == 5 and p_ok:
                            project_outputs((1,))
                        if k == 6 and p_ok:
                            project_outputs((3,))
                        if k == 8 and a_ok:
                            max_columns(O, 0, ahead)
                        if k == 9 and j_ok:
                            project_queries((1,))
                        if k == 10 and j_ok:
                            project_queries((3,))
                        next_maximum(NH)
                        if k == 8 and p_ok and O == 0:
                            transpose_rows()
                return slot

            pe.wait_ge(idd, 3)
            pe.wait_ge(w_in, 16 * NW)
            pe.wait_ge(flag_col, MLOADS + 1)
            nc.tensor.transpose(job[0:1, 0:KCS], mcol[:, :], ident[0:KCS, 0:KCS]).then_inc(flag_row, 1)
            pe.wait_ge(flag_ok, 2)
            any_mask = pe.value_load(mflag[0:1, 0:1], min_val=0, max_val=1)
            with pe.If(any_mask == 0):
                run(pe, slots(False))
            with pe.Else():
                run(pe, slots(True))


def run(eng, slot):
    FIRST, STEADY, LAST = -1, 3, B - 2
    for i in range(FIRST, STEADY):
        for L in range(LAYERS):
            slot(L, i, exists(L, i))
    with eng.Fori(STEADY, LAST) as i:
        for L in range(LAYERS):
            slot(L, i, exists(L, None))
    for i in range(LAST, B + 2):
        for L in range(LAYERS):
            slot(L, i, exists(L, i))


def kernel(**inputs):
    import numpy as np
    import concourse.bacc as bacc
    from concourse.bass_utils import run_bass_kernel_spmd

    nc = bacc.Bacc("TRN2", target_bir_lowering=False, num_devices=1)
    arrays = {}

    def put(name, a):
        a = np.ascontiguousarray(a)
        arrays["in_" + name] = a
        return nc.dram_tensor("in_" + name, a.shape, mybir.dt.from_np(a.dtype), kind="ExternalInput").ap()

    x = np.asarray(inputs["x"])
    c = np.asarray(inputs["ctx_2048"])
    m = np.asarray(inputs["mask_Bx1xSxS2_ff0"])
    xT_d = put("xT", x.reshape(B, S, DC, P).transpose(0, 3, 2, 1).reshape(B, P, DC * S))
    x_d = put("x", x)
    ctxT_d = put("ctxT", c.reshape(B, S2, DC, P).transpose(0, 3, 2, 1).reshape(B, P, DC * S2))
    mask_d = put("mask", m.reshape(B, S, S2))
    mflat_d = put("mask_bits", m.reshape(MLOADS, KCS, MROW).view(np.uint32))
    W = []
    for L in range(LAYERS):
        w = {k: np.asarray(inputs[f"L{L}_xattn_{k}"])
             for k in ("Wq", "bq", "Wk", "bk", "Wv", "bv", "Wo", "bo", "gamma", "beta")}
        W.append({
            "Wq": put(f"Wq{L}", w["Wq"].reshape(DC, P, 2, 4, NG, HD).transpose(1, 0, 4, 2, 5, 3).reshape(P, DC * D)),
            "Wk": put(f"Wk{L}", w["Wk"].reshape(DC, P, 2, 4, HD).transpose(1, 0, 2, 4, 3).reshape(P, DC * P)),
            "Wv": put(f"Wv{L}", w["Wv"].reshape(DC, P, P).transpose(1, 0, 2).reshape(P, DC * P)),
            "Wo": put(f"Wo{L}", w["Wo"].reshape(NKV, NG, HD, D).transpose(0, 2, 1, 3).reshape(P, NG * D)),
            "bq": put(f"bq{L}", w["bq"].reshape(2, 4, NG, HD).transpose(0, 3, 1, 2).reshape(P, NG)),
            "bk": put(f"bk{L}", w["bk"].reshape(2, 4, HD).transpose(0, 2, 1).reshape(P, 1)),
            "bv": put(f"bv{L}", w["bv"].reshape(1, P)),
            "bo": put(f"bo{L}", w["bo"].reshape(1, D)),
            "gamma": put(f"gamma{L}", w["gamma"].reshape(1, D)),
            "beta": put(f"beta{L}", w["beta"].reshape(1, D)),
        })
    out = nc.dram_tensor("out", (B, S, D), F32, kind="ExternalOutput").ap()
    cross_attention_two_layers(nc, xT_d, x_d, ctxT_d, mask_d, mflat_d, W, out)
    r = run_bass_kernel_spmd(nc, [arrays], core_ids=[0])
    return r.results[0]["out"]
```
